# Optimizing a Trainium2 kernel written in Bass

```python
import numpy as np
import jax
import jax.numpy as jnp

def _softmax(x, axis=-1):
    return jax.nn.softmax(x, axis=axis)

def _gelu(x):
    return jax.nn.gelu(x, approximate=True)

def _silu(x):
    return jax.nn.silu(x)

def _sigmoid(x):
    return jax.nn.sigmoid(x)

def _layernorm(x, axis=-1, eps=1e-05):
    m = jnp.mean(x, axis=axis, keepdims=True)
    v = jnp.var(x, axis=axis, keepdims=True)
    return (x - m) / jnp.sqrt(v + eps)

def _scatter_add(tgt, idx, src, axis=0):
    return tgt.at[idx].add(src)

def _segment_sum(src, seg, n):
    return jax.ops.segment_sum(src, seg, n)
kernel_name = 'mk_cond_resid_d4_seqx_r8_5b4a4c'

def setup_inputs(seed: int=0):
    np.random.seed(seed)
    _w = jnp.asarray

    def _rec_inputs():
        import jax
        import jax.numpy as jnp
        _rk = jax.random.key(seed)
        x = -7.109e-05 + 0.9999 * jax.random.normal(jax.random.fold_in(_rk, 1), (8, 128, 512), jnp.float32)
        _lenS = 128 - jax.random.randint(jax.random.fold_in(_rk, 7), (8,), 0, max(1, 128 // 4) + 1, jnp.int32)
        _lenS2 = 128 - jax.random.randint(jax.random.fold_in(_rk, 8), (8,), 0, max(1, 128 // 4) + 1, jnp.int32)
        itok_B_0_15 = jax.random.randint(jax.random.fold_in(_rk, 11), (8,), 0, 16, jnp.int32)
        itok_B_0_7 = jax.random.randint(jax.random.fold_in(_rk, 12), (8,), 0, 8, jnp.int32)
        itok_B_0_4 = jax.random.randint(jax.random.fold_in(_rk, 13), (8,), 0, 5, jnp.int32)
        itok_B_2_6 = jax.random.randint(jax.random.fold_in(_rk, 14), (8,), 2, 7, jnp.int32)
        return (x, itok_B_0_15, itok_B_0_7, itok_B_0_4, itok_B_2_6)
    x, itok_B_0_15, itok_B_0_7, itok_B_0_4, itok_B_2_6 = _rec_inputs()

    def _L0_cond_setup():
        import jax, jax.numpy as jnp
        import numpy as np
        MAX_LORAS = 16
        IN, OUT = (512, 512)
        B, S = (8, 256)
        key = jax.random.key(seed)
        k1, k2, k3 = jax.random.split(key, 3)
        x = jax.random.normal(k1, (B, S, IN), dtype=jnp.float32)
        adapter_ids = jax.random.randint(k2, (B,), 0, MAX_LORAS)
        weight = jax.random.normal(k3, (MAX_LORAS, OUT, IN), dtype=jnp.float32) * 0.02
        return {'x': x, 'adapter_ids': adapter_ids, 'weight': weight}
    _L0_cond_all = _L0_cond_setup()
    _L0_cond_in = {k: v for k, v in _L0_cond_all.items() if k in ('weight',)}
    del _L0_cond_all

    def _L1_cond_setup():
        import jax, jax.numpy as jnp
        import numpy as np
        TOP_K = 2
        LANG_BIAS = 5.0
        SCALING = 32.0 / 16.0
        LANGUAGE_PAD_ID = -1
        key = jax.random.key(seed)
        ks = jax.random.split(key, 6)
        B, T, D, O, E, R = (4, 256, 512, 512, 8, 16)
        x = jax.random.normal(ks[0], (B, T, D), dtype=jnp.float32)
        language_ids = jax.random.randint(ks[1], (B,), 0, E).astype(jnp.int64)
        W = jax.random.normal(ks[2], (O, D), dtype=jnp.float32) * (1.0 / np.sqrt(D))
        Wr = jax.random.normal(ks[3], (E, D), dtype=jnp.float32) * (1.0 / np.sqrt(D))
        A = jax.random.normal(ks[4], (E, R, D), dtype=jnp.float32) * (1.0 / np.sqrt(D))
        Bm = jax.random.normal(ks[5], (O, R), dtype=jnp.float32) * 0.0
        Bm = jnp.broadcast_to(Bm, (E, O, R)) + jax.random.normal(ks[5], (E, O, R), dtype=jnp.float32) * 0.02
        return {'x': x, 'language_ids': language_ids, 'W': W, 'Wr': Wr, 'A': A, 'B': Bm}
    _L1_cond_all = _L1_cond_setup()
    _L1_cond_in = {k: v for k, v in _L1_cond_all.items() if k in ('W', 'Wr', 'A', 'B')}
    del _L1_cond_all

    def _L2_cond_setup():
        import jax, jax.numpy as jnp
        import numpy as np
        B, S, D_IN, D_OUT = (8, 256, 512, 512)
        R, NUM_LABELERS = (32, 5)
        LORA_SCALING = 16 / 32
        key = jax.random.key(seed)
        k1, k2, k3, k4, k5, k6 = jax.random.split(key, 6)
        inp = {'input': jax.random.normal(k1, (B, S, D_IN), dtype=jnp.float32), 'weight': jax.random.normal(k2, (D_OUT, D_IN), dtype=jnp.float32) * 0.02, 'bias': jax.random.normal(k3, (D_OUT,), dtype=jnp.float32) * 0.02, 'lora_A': jax.random.normal(k4, (NUM_LABELERS, D_IN, R), dtype=jnp.float32) * 0.02, 'lora_B': jax.random.normal(k5, (D_OUT, R), dtype=jnp.float32) * 0.02, 'labeler_index': jax.random.randint(k6, (B,), 0, NUM_LABELERS, dtype=jnp.int64) if jax.config.jax_enable_x64 else jax.random.randint(k6, (B,), 0, NUM_LABELERS, dtype=jnp.int32)}
        return inp
    _L2_cond_all = _L2_cond_setup()
    _L2_cond_in = {k: v for k, v in _L2_cond_all.items() if k in ('weight', 'bias', 'lora_A', 'lora_B')}
    del _L2_cond_all

    def _L3_cond_setup():
        import jax, jax.numpy as jnp
        import numpy as np
        B, N, H, F = (4, 64, 512, 1376)
        L, R, RANK = (1, 16, 16)
        SCALE = 0.5
        key = jax.random.key(seed)
        ks = jax.random.split(key, 12)
        nrm = lambda k, shape, fan: jax.random.normal(k, shape, jnp.float32) * fan ** (-0.5)
        inp = {'x': jax.random.normal(ks[0], (B, N, H), jnp.float32), 'W_gate': nrm(ks[1], (F, H), H), 'W_up': nrm(ks[2], (F, H), H), 'W_down': nrm(ks[3], (H, F), F), 'A_gate': nrm(ks[4], (L, R, RANK, H), H), 'B_gate': nrm(ks[5], (L, R, F, RANK), RANK), 'A_up': nrm(ks[6], (L, R, RANK, H), H), 'B_up': nrm(ks[7], (L, R, F, RANK), RANK), 'A_down': nrm(ks[8], (L, R, RANK, F), F), 'B_down': nrm(ks[9], (L, R, H, RANK), RANK), 'lora_indices': jax.random.randint(ks[10], (B,), 0, R), 'layer_idx': 0}
        return inp
    _L3_cond_all = _L3_cond_setup()
    _L3_cond_in = {k: v for k, v in _L3_cond_all.items() if k in ('W_gate', 'W_up', 'W_down', 'A_gate', 'B_gate', 'A_up', 'B_up', 'A_down', 'B_down')}
    del _L3_cond_all
    return {'x': x, 'itok_B_0_15': itok_B_0_15, 'itok_B_0_7': itok_B_0_7, 'itok_B_0_4': itok_B_0_4, 'itok_B_2_6': itok_B_2_6, 'L0_cond_weight': _L0_cond_in['weight'], 'L1_cond_W': _L1_cond_in['W'], 'L1_cond_Wr': _L1_cond_in['Wr'], 'L1_cond_A': _L1_cond_in['A'], 'L1_cond_B': _L1_cond_in['B'], 'L2_cond_weight': _L2_cond_in['weight'], 'L2_cond_bias': _L2_cond_in['bias'], 'L2_cond_lora_A': _L2_cond_in['lora_A'], 'L2_cond_lora_B': _L2_cond_in['lora_B'], 'L3_cond_W_gate': _L3_cond_in['W_gate'], 'L3_cond_W_up': _L3_cond_in['W_up'], 'L3_cond_W_down': _L3_cond_in['W_down'], 'L3_cond_A_gate': _L3_cond_in['A_gate'], 'L3_cond_B_gate': _L3_cond_in['B_gate'], 'L3_cond_A_up': _L3_cond_in['A_up'], 'L3_cond_B_up': _L3_cond_in['B_up'], 'L3_cond_A_down': _L3_cond_in['A_down'], 'L3_cond_B_down': _L3_cond_in['B_down']}

def reference(x, itok_B_0_15, itok_B_0_7, itok_B_0_4, itok_B_2_6, L0_cond_weight, L1_cond_W, L1_cond_Wr, L1_cond_A, L1_cond_B, L2_cond_weight, L2_cond_bias, L2_cond_lora_A, L2_cond_lora_B, L3_cond_W_gate, L3_cond_W_up, L3_cond_W_down, L3_cond_A_gate, L3_cond_B_gate, L3_cond_A_up, L3_cond_B_up, L3_cond_A_down, L3_cond_B_down):
    import jax
    import jax.numpy as jnp

    def _L0_cond_ref(x, adapter_ids, weight):
        import jax, jax.numpy as jnp
        import numpy as np
        MAX_LORAS = 16
        IN, OUT = (512, 512)
        B, S = (8, 256)
        w = weight[adapter_ids]
        return jnp.einsum('bsi,boi->bso', x, w)

    def _L1_cond_ref(x, language_ids, W, Wr, A, B):
        import jax, jax.numpy as jnp
        import numpy as np
        TOP_K = 2
        LANG_BIAS = 5.0
        SCALING = 32.0 / 16.0
        LANGUAGE_PAD_ID = -1
        base = jnp.einsum('btd,od->bto', x, W)
        E = Wr.shape[0]
        logits = jnp.einsum('btd,ed->bte', x.astype(jnp.float32), Wr.astype(jnp.float32))
        expert_targets = language_ids
        valid = expert_targets >= 0
        tgt = jnp.where(valid, expert_targets, 0)
        bias = jax.nn.one_hot(tgt, E, dtype=logits.dtype) * LANG_BIAS
        bias = jnp.where(valid[:, None], bias, 0.0)
        logits = logits + bias[:, None, :]
        topw, topi = jax.lax.top_k(logits, TOP_K)
        weights = jax.nn.softmax(topw, axis=-1)
        gates = jnp.sum(jax.nn.one_hot(topi, E, dtype=weights.dtype) * weights[..., None], axis=-2)
        gates = gates.astype(x.dtype)
        h = jnp.einsum('btd,erd->bter', x, A)
        lora_out = jnp.einsum('bter,bte,eor->bto', h, gates, B)
        return base + SCALING * lora_out

    def _L2_cond_ref(input, weight, bias, lora_A, lora_B, labeler_index):
        import jax, jax.numpy as jnp
        import numpy as np
        B, S, D_IN, D_OUT = (8, 256, 512, 512)
        R, NUM_LABELERS = (32, 5)
        LORA_SCALING = 16 / 32
        base = jnp.einsum('bsi,oi->bso', input, weight) + bias
        labelers_A = lora_A[labeler_index]
        ax = jnp.einsum('bsi,bir->bsr', input, labelers_A)
        delta = jnp.einsum('bsr,or->bso', ax, lora_B)
        return base + delta * LORA_SCALING

    def _L3_cond_ref(x, W_gate, W_up, W_down, A_gate, B_gate, A_up, B_up, A_down, B_down, lora_indices, layer_idx):
        import jax, jax.numpy as jnp
        import numpy as np
        B, N, H, F = (4, 64, 512, 1376)
        L, R, RANK = (1, 16, 16)
        SCALE = 0.5

        def lora_add(base, inp, A, B):
            Ab = A[layer_idx][lora_indices]
            Bb = B[layer_idx][lora_indices]
            t = jnp.einsum('bri,bni->bnr', Ab, inp)
            return base + jnp.einsum('bor,bnr->bno', Bb, t) * SCALE
        gate = lora_add(jnp.einsum('bnh,fh->bnf', x, W_gate), x, A_gate, B_gate)
        up = lora_add(jnp.einsum('bnh,fh->bnf', x, W_up), x, A_up, B_up)
        act = jax.nn.silu(gate) * up
        down = lora_add(jnp.einsum('bnf,hf->bnh', act, W_down), act, A_down, B_down)
        return down
    x = x + _L0_cond_ref(x, itok_B_0_15, L0_cond_weight)
    x = x + _L1_cond_ref(x, itok_B_0_7, L1_cond_W, L1_cond_Wr, L1_cond_A, L1_cond_B)
    x = x + _L2_cond_ref(x, L2_cond_weight, L2_cond_bias, L2_cond_lora_A, L2_cond_lora_B, itok_B_0_4)
    x = x + _L3_cond_ref(x, L3_cond_W_gate, L3_cond_W_up, L3_cond_W_down, L3_cond_A_gate, L3_cond_B_gate, L3_cond_A_up, L3_cond_B_up, L3_cond_A_down, L3_cond_B_down, itok_B_2_6, 0)
    return x

_drawn_inputs = setup_inputs


def setup_inputs(seed=0):
    import zlib

    import numpy as np

    out = dict(_drawn_inputs(seed))
    spreads = {}
    factors = {'L1_cond_Wr': 3.28, 'L2_cond_bias': 3.813}
    for name, (base, spread) in spreads.items():
        noise = np.random.default_rng([zlib.crc32(name.encode()), seed]).standard_normal(out[name].shape)
        drawn = base * np.exp(spread * noise) if base else spread * noise
        out[name] = jnp.asarray(drawn.astype(out[name].dtype))
    for name, factor in factors.items():
        out[name] = (out[name] * factor).astype(out[name].dtype)
    return out
```

```python
from contextlib import ExitStack

import concourse.bass as bass
from concourse import mybir

F32 = mybir.dt.float32
F32R = mybir.dt.float32r
I32 = mybir.dt.int32
U32 = mybir.dt.uint32
ALU = mybir.AluOpType
ACT = mybir.ActivationFunctionType
AX_X = mybir.AxisListType.X

P = 128
B, S, D = 8, 128, 512
C = D // P
T = B * S
H = 2
HB = B // H
HT = T // H
E, R = 8, 16
ER = E * R
TM1 = ER + E
R2 = 32
RG = 2 * R
FC = 11
LANG_BIAS = 5.0
SCALING1 = 2.0
SCALING = 0.5
BANK = 512
RAWC = C - 1
KC = C - 1
W0_RING = 3
WD_RING = 4


def bass_four_residual_layers(nc, xT, ids0, ids1, ids2, ids3, w0, w1, aw1, b1, w2, a2, b2, bias2,
                              wgu, agu, bgu, wd, ad, bd, out):
    ctx = ExitStack()
    with ctx:
        base = (nc.sbuf_base + 31) // 32 * 32

        def at(name, off, shape, dt=F32):
            return nc.alloc_sbuf_tensor_at(name, [P, *shape], dt, offset=base + off)

        KB = 1024
        o_xf, o_xb, o_act = 0, 16 * KB, 48 * KB
        o_xa = o_act
        o_w0 = o_act + 32 * KB
        o_w1 = o_act + 56 * KB
        o_w2 = o_act + 72 * KB
        o_wgu = 136 * KB
        o_raw = o_wgu + 16 * KB
        o_slot2 = o_raw + 16 * KB
        o_bst = o_slot2 + 8 * KB
        o_tp = o_bst + 8 * KB
        o_ad = o_tp + 8 * KB
        o_misc = o_ad + 11 * KB

        x_f = at("x_f", o_xf, [C, T])
        xa = at("xa", o_xa, [2, C, T], F32R)
        xb = at("xb", o_xb, [2, C, T], F32R)
        w0_raw = [at(f"w0_raw{i}", o_raw + i * 8 * KB, [C, D]) for i in range(W0_RING)]
        w0_hl = [at(f"w0_hl{i}", (o_w0, o_w0 + 12 * KB, o_w2)[i], [2, KC, D], F32R)
                 for i in range(W0_RING)]
        y0 = [at(f"y0_{i}", o_tp + i * 2 * KB, [D]) for i in range(2)]
        w1_raw = at("w1_raw", o_slot2, [C, C, P])
        w1_hl = at("w1_hl", o_w1, [2, C, C, P], F32R)
        aw1_hl = at("aw1_hl", o_wgu, [C, 2, TM1], F32R)
        b1_hl = at("b1_hl", o_wgu + 5 * KB, [2, D], F32R)
        aw1_raw = at("aw1_raw", o_bst, [C, TM1])
        b1_raw = at("b1_raw", o_bst + 3 * KB, [D])
        h_sum = [at(f"h_sum{i}", o_w0 + i * 3 * KB, [HB, TM1]) for i in range(H)]
        h_gated = [at(f"h_gated{i}", o_w0 + 20 * KB + i * 2 * KB, [HB, ER]) for i in range(H)]
        hg_hl = at("hg_hl", o_w0 + 12 * KB, [2, T], F32R)
        w2_raw = at("w2_raw", o_raw, [C, C, P])
        w2_hl = at("w2_hl", o_w2, [2, C, C, P], F32R)
        a2_raw = at("a2_raw", o_tp + 4 * KB, [B, C, R2])
        a2_hl = at("a2_hl", o_ad, [B, C, 2, R2], F32R)
        b2_raw = at("b2_raw", o_bst + 5 * KB, [D])
        b2_st = at("b2_st", o_ad + 8 * KB, [D], F32R)
        t2_parts = [at(f"t2_parts{i}", o_w0 + 20 * KB + i * 2 * KB, [HB, 4, R2]) for i in range(H)]
        t2_st = at("t2_st", o_tp, [T], F32R)
        agu_raw = at("agu_raw", o_w0 + 8 * KB, [B, C, RG])
        agu_hl = at("agu_hl", o_w0, [B, C, 2, RG], F32R)
        t3_parts = [at(f"t3_parts{i}", o_slot2 + i * 4 * KB, [HB, 2, P]) for i in range(H)]
        t3_st = at("t3_st", o_tp, [2, T], F32R)
        bgu_raw = [at(f"bgu_raw{i}", o_raw + i * 4 * KB, [B // 2, 2, P]) for i in range(2)]
        wgu_raw = [at(f"wgu_raw{i}", o_raw + (8 + i * 4) * KB, [C, 2, P]) for i in range(2)]
        bgu_st = [at(f"bgu_st{i}", o_bst + i * 4 * KB, [B // 2, 2, P], F32R) for i in range(2)]
        wgu_hl = [at(f"wgu_hl{i}", o_wgu + i * 8 * KB, [2, C, 2, P], F32R) for i in range(2)]
        act_hl = at("act_hl", o_act, [FC, 2, T], F32R)
        ad_raw = at("ad_raw", o_act + 80 * KB, [B, FC, R])
        ad_hl = at("ad_hl", o_ad, [B, FC, 2, R], F32R)
        wd_lo_places = [o_slot2, o_slot2 + 4 * KB] + [o_xb + i * 4 * KB for i in range(8)] + [o_bst]
        wd_hl = [at(f"wd_hl{f}", wd_lo_places[f], [2, D], F32R) for f in range(FC)]
        bd_raw = at("bd_raw", o_raw, [B // 2, D])
        bd_st = at("bd_st", o_wgu, [B // 2, D], F32R)
        y_out = [at(f"y_out{i}", o_wgu + (8 + 2 * i) * KB, [D]) for i in range(2)]
        m = [o_misc]

        def own(name, shape, dt=F32):
            n = 4
            for k in shape:
                n *= k
            t = at(name, m[0], shape, dt)
            m[0] += (n + 31) // 32 * 32
            return t

        ident = own("ident", [P])
        wd_raw = [own(f"wd_raw{i}", [D]) for i in range(WD_RING)]
        act_f = [own(f"act_f{i}", [HT]) for i in range(2)]
        td_parts = [own(f"td_parts{i}", [P]) for i in range(2)]
        td_st = [own(f"td_st{i}", [P], F32R) for i in range(2)]
        td_f = [own(f"td_f{i}", [R]) for i in range(2)]
        t23_f = [own(f"t23_f{i}", [HB, RG]) for i in range(2)]
        bias_sb = own("bias_sb", [C])
        lo_rows32 = own("lo_rows32", [1])
        lo_rows16 = own("lo_rows16", [1])
        lang_i = own("lang_i", [B], I32)
        lang_f = own("lang_f", [B])
        iota_e = own("iota_e", [E])
        lang_bias = own("lang_bias", [B, E])
        logits = own("logits", [HB, E])
        top_v = own("top_v", [HB, 8])
        top_i = own("top_i", [HB, 8], U32)
        top_f = own("top_f", [HB, 2])
        gap = own("gap", [HB])
        gap_e = own("gap_e", [HB])
        gate_w = own("gate_w", [4, HB])
        eq = own("eq", [2, HB, E])
        assert base + m[0] <= nc.sbuf_usable_end, (base + m[0], nc.sbuf_usable_end)

        bank = [ctx.enter_context(nc.psum_tensor(f"bank{i}", [P, BANK], F32)) for i in range(8)]

        def sem(name):
            return ctx.enter_context(nc.semaphore(name))

        x_in = [sem(f"x_in{b}") for b in range(B)]
        w0c_in = [sem(f"w0c_in{c}") for c in range(C)]
        w0_in = [sem(f"w0_in{i}") for i in range(W0_RING)]
        aw1_in, b1_in, lang_in = sem("aw1_in"), sem("b1_in"), sem("lang_in")
        w1_in = [sem(f"w1_in{o}") for o in range(C)]
        w2_in, a2_in, b2_in, bias_in = sem("w2_in"), sem("a2_in"), sem("b2_in"), sem("bias_in")
        agu_in = sem("agu_in")
        wgu_in = [sem(f"wgu_in{i}") for i in range(2)]
        bgu_in = [sem(f"bgu_in{i}") for i in range(2)]
        ad_in, bd_in = sem("ad_in"), sem("bd_in")
        wd_in = [sem(f"wd_in{i}") for i in range(WD_RING)]
        out_sent = [sem(f"out_sent{i}") for i in range(2)]
        const_step, ident_ready, masks_ready, iota_ready = (sem(n) for n in (
            "const_step", "ident_ready", "masks_ready", "iota_ready"))
        t3_zeroed, td_zeroed = sem("t3_zeroed"), sem("td_zeroed")
        x0_hi, x0_lo = sem("x0_hi"), sem("x0_lo")
        w0_raw_used, l0_tm, l0_tr = sem("w0_raw_used"), sem("l0_tm"), sem("l0_tr")
        l1_tm, l1_tr = sem("l1_tm"), sem("l1_tr")
        l2_tm, l2_tr = sem("l2_tm"), sem("l2_tr")
        l3_tm, l3_tr = sem("l3_tm"), sem("l3_tr")
        main_done = sem("main_done")
        gate_done, up_done = sem("gate_done"), sem("up_done")
        td_done, td_tr, down_done = sem("td_done"), sem("td_tr"), sem("down_done")
        w0_hi, y0_copied, x1_hi = sem("w0_hi"), sem("y0_copied"), sem("x1_hi")
        w12_hi, gap_exp, hg_hi = sem("w12_hi"), sem("gap_exp"), sem("hg_hi")
        x_hi, t2_copied, t3_copied = sem("x_hi"), sem("t2_copied"), sem("t3_copied")
        wgu_hi, bgu_hi, silu_done, act_hi = sem("wgu_hi"), sem("bgu_hi"), sem("silu_done"), sem("act_hi")
        ad_hi, wd_hi, bd_hi = sem("ad_hi"), sem("wd_hi"), sem("bd_hi")
        td_copied, out_copied = sem("td_copied"), sem("out_copied")
        w0_lo, x1_sum, x1_lo = sem("w0_lo"), sem("x1_sum"), sem("x1_lo")
        w12_lo, router_step, gap_ready, h_gated_ready = (sem(n) for n in (
            "w12_lo", "router_step", "gap_ready", "h_gated_ready"))
        hg_lo, x_sum, x_lo = sem("hg_lo"), sem("x_sum"), sem("x_lo")
        thin_sum, thin_hi, t2_ready, t3_ready = (sem(n) for n in (
            "thin_sum", "thin_hi", "t2_ready", "t3_ready"))
        wgu_lo, bgu_ready, act_mul, act_lo = sem("wgu_lo"), sem("bgu_ready"), sem("act_mul"), sem("act_lo")
        ad_lo, wd_lo, bd_ready = sem("ad_lo"), sem("wd_lo"), sem("bd_ready")
        td_sum, td_hi, td_ready = sem("td_sum"), sem("td_hi"), sem("td_ready")

        def w0_landed(b):
            return 16 * (b // W0_RING + (b % W0_RING > 0))

        def number(l, h, o):
            return 8 * (l - 1) + C * h + o

        splits = ["aw1"] + [f"w1_{o}" for o in range(C)] + ["b1", "a2"] + [f"w2_{o}" for o in range(C)] + ["b2", "agu"]
        nth = {name: i + 1 for i, name in enumerate(splits)}

        def split_views(name):
            if name == "aw1":
                return aw1_raw[:], aw1_hl[:, :, 0], aw1_hl[:, :, 1]
            if name == "b1":
                return b1_raw[:], b1_hl[:, 0], b1_hl[:, 1]
            if name == "a2":
                return a2_raw[:], a2_hl[:, :, :, 0], a2_hl[:, :, :, 1]
            if name == "agu":
                return agu_raw[:], agu_hl[:, :, :, 0], agu_hl[:, :, :, 1]
            if name == "b2":
                return b2_raw[:], b2_st[:], b2_st[:]
            raw, hl = (w1_raw, w1_hl) if name[1] == "1" else (w2_raw, w2_hl)
            o = int(name[3:])
            return raw[:, o], hl[:, 0, o], hl[:, 1, o]

        split_source = {"aw1": (aw1_in, 16), "b1": (b1_in, 16), "a2": (a2_in, 16 * B), "agu": (agu_in, 16 * B),
                        "b2": (b2_in, 16)}
        for o in range(C):
            split_source[f"w1_{o}"] = (w1_in[o], 16)
            split_source[f"w2_{o}"] = (w2_in, 16)

        block = ctx.enter_context(nc.Block())

        @block.sync
        def _(sp):
            def id_of(src, b, last):
                return sp.value_load(src[0:1, b:b + 1], min_val=0, max_val=last)

            sp.dma_start(x_f[:, :, 0:S], xT[0]).then_inc(x_in[0], 16)
            adapter = id_of(ids0, 0, w0.shape[0] - 1)
            for c in range(C):
                sp.dma_start(w0_raw[0][:, c], w0[adapter][:, c * D:(c + 1) * D]).then_inc(w0c_in[c], 16)
            for b in range(1, B):
                sp.dma_start(x_f[:, :, b * S:(b + 1) * S], xT[b]).then_inc(x_in[b], 16)
                adapter = id_of(ids0, b, w0.shape[0] - 1)
                if b == W0_RING:
                    sp.wait_ge(l0_tm, 1)
                if b > W0_RING:
                    sp.wait_ge(w0_raw_used, b - W0_RING)
                    sp.wait_ge(w0_lo, b - W0_RING)
                sp.dma_start(w0_raw[b % W0_RING][:], w0[adapter]).then_inc(w0_in[b % W0_RING], 16)
                if b == 4:
                    sp.dma_start(aw1_raw[:], aw1).then_inc(aw1_in, 16)
                    sp.dma_start(lang_i[:], ids1.partition_broadcast(P)).then_inc(lang_in, 16)
            sp.wait_ge(w0_raw_used, 5)
            sp.wait_ge(w0_lo, 5)
            for o in range(C):
                sp.dma_start(w1_raw[:, o], w1[:, o]).then_inc(w1_in[o], 16)
            sp.dma_start(b1_raw[:], b1).then_inc(b1_in, 16)
            for b in range(B):
                sp.dma_start(a2_raw[:, b], a2[id_of(ids2, b, a2.shape[0] - 1)]).then_inc(a2_in, 16)
            sp.dma_start(b2_raw[:], b2).then_inc(b2_in, 16)
            sp.dma_start(bias_sb[:], bias2).then_inc(bias_in, 16)
            sp.wait_ge(w0_raw_used, 7)
            sp.wait_ge(w0_lo, 7)
            sp.dma_start(w2_raw[:], w2).then_inc(w2_in, 16)
            adapter3 = [id_of(ids3, b, agu.shape[0] - 1) for b in range(B)]
            sp.wait_ge(l0_tm, 8)
            for b in range(B):
                sp.dma_start(agu_raw[:, b], agu[adapter3[b]]).then_inc(agu_in, 16)

            def load_gate_up(fc, slot):
                sp.dma_start(wgu_raw[slot][:], wgu[fc]).then_inc(wgu_in[slot], 16)
                for b in range(B):
                    rows = slice(64 * (b % 2), 64 * (b % 2) + 64)
                    sp.dma_start(bgu_raw[slot][rows, b // 2], bgu[adapter3[b], fc]).then_inc(bgu_in[slot], 16)

            sp.wait_ge(w12_lo, nth["w2_3"])
            load_gate_up(0, 0)
            load_gate_up(1, 1)
            with sp.Fori(0, 4) as i:
                for u in range(2):
                    fc = 2 * i + 2 + u
                    sp.wait_ge(wgu_lo, 2 * i + 1 + u)
                    sp.wait_ge(bgu_ready, 2 * i + 1 + u)
                    load_gate_up(fc, u)
            sp.wait_ge(wgu_lo, FC - 2)
            sp.wait_ge(bgu_ready, FC - 2)
            load_gate_up(FC - 1, 0)
            for b in range(B):
                sp.dma_start(ad_raw[:, b], ad[adapter3[b]]).then_inc(ad_in, 16)
            for f in range(FC):
                if f >= WD_RING:
                    sp.wait_ge(wd_lo, f - WD_RING + 1)
                sp.dma_start(wd_raw[f % WD_RING][:], wd[:, f]).then_inc(wd_in[f % WD_RING], 16)
                if f == WD_RING:
                    sp.wait_ge(bgu_ready, FC)
                    sp.wait_ge(wgu_lo, FC)
                    for b in range(B):
                        rows = slice(64 * (b % 2), 64 * (b % 2) + 64)
                        sp.dma_start(bd_raw[rows, b // 2], bd[adapter3[b]]).then_inc(bd_in, 16)
            for b in range(B):
                sp.wait_ge(out_copied, b + 1)
                sp.dma_start(out[b], y_out[b % 2][:]).then_inc(out_sent[b % 2], 16)
            for i in range(2):
                sp.wait_ge(out_sent[i], 16 * B // 2)

        @block.gpsimd
        def _(pool):
            pool.memset(ident[:], 0.0).then_inc(const_step, 1)
            pool.wait_ge(const_step, 1)
            pool.affine_select(out=ident[:], in_=ident[:], compare_op=ALU.not_equal, fill=1.0, base=0,
                               pattern=[[-1, P]], channel_multiplier=1).then_inc(ident_ready, 1)
            pool.iota(iota_e[:], [[1, E]], base=0, channel_multiplier=0,
                      allow_small_or_imprecise_dtypes=True).then_inc(iota_ready, 1)
            pool.memset(td_parts[0][:], 0.0)
            pool.memset(td_parts[1][:], 0.0).then_inc(td_zeroed, 1)
            for b in range(1, B):
                cols = slice(b * S, (b + 1) * S)
                pool.wait_ge(x_in[b], 16)
                pool.tensor_copy(xa[:, 0, 0:KC, cols], x_f[:, 0:KC, cols]).then_inc(x0_hi, 1)
                pool.wait_ge(x0_hi, b)
                pool.tensor_tensor(xa[:, 1, 0:KC, cols], x_f[:, 0:KC, cols],
                                   xa[:, 0, 0:KC, cols].bitcast(F32), ALU.subtract).then_inc(x0_lo, 1)
            pool.wait_ge(w12_lo, nth["w1_3"])
            pool.memset(t3_parts[0][:], 0.0)
            pool.memset(t3_parts[1][:], 0.0).then_inc(t3_zeroed, 1)

        @block.scalar
        def _(act):
            def high(dst, src):
                return act.activation(dst, src, ACT.Copy)

            def split_hi(name):
                s, n = split_source[name]
                act.wait_ge(s, n)
                raw, hi, _ = split_views(name)
                high(hi, raw).then_inc(w12_hi, 1)

            def copy_y0(b):
                act.wait_ge(l0_tm, b + 1)
                if b >= 2:
                    act.wait_ge(l0_tr, b - 1)
                act.activation(y0[b % 2][:], bank[b % 2][:], ACT.Copy).then_inc(y0_copied, 1)

            def x1_high(b):
                cols = slice(b * S, (b + 1) * S)
                act.wait_ge(x1_sum, b + 1)
                high(xb[:, 0, :, cols], x_f[:, :, cols]).then_inc(x1_hi, 1)

            for b in range(1, B):
                act.wait_ge(w0_in[b % W0_RING], w0_landed(b))
                if b > W0_RING:
                    act.wait_ge(l0_tm, b - W0_RING + 1)
                high(w0_hl[b % W0_RING][:, 0], w0_raw[b % W0_RING][:, 0:KC]).then_inc(w0_hi, 1)
                if b >= 2:
                    copy_y0(b - 2)
                if b >= 4:
                    x1_high(b - 4)
                if b == 6:
                    split_hi("aw1")
            copy_y0(6)
            x1_high(4)
            copy_y0(7)
            x1_high(5)
            split_hi("w1_0")
            x1_high(6)
            x1_high(7)
            for o in range(1, C):
                split_hi(f"w1_{o}")
            split_hi("b1")

            def router_exp(h):
                act.wait_ge(gap_ready, h + 1)
                act.activation(gap_e[:], gap[:], ACT.Exp).then_inc(gap_exp, 1)

            def hg_high(h):
                act.wait_ge(l1_tr, h + 1)
                high(hg_hl[:, 0, h * HT:(h + 1) * HT], bank[0][:]).then_inc(hg_hi, 1)

            def x_high(l, h, o):
                n = number(l, h, o)
                dst = (xa if l == 1 else xb)[:, 0, o, h * HT:(h + 1) * HT]
                act.wait_ge(x_sum, n + 1)
                high(dst, x_f[:, o, h * HT:(h + 1) * HT]).then_inc(x_hi, 1)

            router_exp(0)
            split_hi("a2")
            hg_high(0)
            for o in range(C):
                x_high(1, 0, o)
                split_hi(f"w2_{o}")
            router_exp(1)
            hg_high(1)
            split_hi("b2")
            for o in range(C):
                x_high(1, 1, o)

            def t2_copy(h):
                act.wait_ge(l2_tr, h + 1)
                act.activation(t2_st[:, h * HT:(h + 1) * HT], bank[2 + h][:], ACT.Copy,
                               scale=SCALING).then_inc(t2_copied, 1)

            def gate_up_hi(fc, slot, uses, free):
                act.wait_ge(wgu_in[slot], 16 * uses)
                if free is not None:
                    act.wait_ge(up_done, free)
                high(wgu_hl[slot][:, 0], wgu_raw[slot][:]).then_inc(wgu_hi, 1)
                act.wait_ge(bgu_in[slot], 16 * B * uses)
                high(bgu_st[slot][:], bgu_raw[slot][:]).then_inc(bgu_hi, 1)

            t2_copy(0)
            split_hi("agu")
            for o in range(C):
                x_high(2, 0, o)
            t2_copy(1)
            gate_up_hi(0, 0, 1, None)
            gate_up_hi(1, 1, 1, None)
            for o in range(C):
                x_high(2, 1, o)

            def t3_copy(h):
                act.wait_ge(l3_tr, h + 1)
                for g in range(2):
                    last = act.activation(t3_st[:, g, h * HT:(h + 1) * HT], bank[2 + g][:], ACT.Copy,
                                          scale=SCALING)
                last.then_inc(t3_copied, 1)

            def silu_and_high(fc, h):
                n = 2 * fc + h
                act.wait_ge(gate_done, n + 1)
                act.activation(act_f[h][:], bank[4 + 2 * h][:], ACT.Silu).then_inc(silu_done, 1)
                act.wait_ge(act_mul, n + 1)
                high(act_hl[:, fc, 0, h * HT:(h + 1) * HT], act_f[h][:]).then_inc(act_hi, 1)

            def down_hi(f):
                act.wait_ge(wd_in[f % WD_RING], 16 * (f // WD_RING + 1))
                high(wd_hl[f][:, 0], wd_raw[f % WD_RING][:]).then_inc(wd_hi, 1)

            t3_copy(0)
            silu_and_high(0, 0)
            t3_copy(1)
            silu_and_high(0, 1)
            with act.Fori(0, 4) as i:
                for u in range(2):
                    fc = 2 * i + 1 + u
                    gate_up_hi(fc + 1, u, i + 2 if u == 0 else i + 2, 4 * i + 2 + 2 * u)
                    for h in range(H):
                        if h == 0:
                            act.wait_ge(act_lo, 2 * fc - 1)
                        else:
                            act.wait_ge(act_lo, 2 * fc)
                        silu_and_high(fc, h)
            act.wait_ge(ad_in, 16 * B)
            high(ad_hl[:, :, :, 0], ad_raw[:]).then_inc(ad_hi, 1)
            gate_up_hi(FC - 1, 0, 6, 2 * (FC - 2))
            act.wait_ge(t3_copied, 2)
            for fc in (FC - 2, FC - 1):
                down_hi(fc - (FC - 2))
                for h in range(H):
                    act.wait_ge(act_lo, 2 * fc - 1 + h)
                    silu_and_high(fc, h)
            act.wait_ge(up_done, 2 * FC)
            for f in range(2, FC):
                down_hi(f)
            act.wait_ge(bd_in, 16 * B)
            high(bd_st[:], bd_raw[:]).then_inc(bd_hi, 1)

            def td_copy(b):
                act.wait_ge(td_tr, b + 1)
                act.activation(td_st[b % 2][:], bank[2 + b % 2][:, 0:S], ACT.Copy,
                               scale=SCALING).then_inc(td_copied, 1)

            def out_copy(b):
                act.wait_ge(down_done, b + 1)
                if b >= 2:
                    act.wait_ge(out_sent[b % 2], 16 * (b // 2))
                act.activation(y_out[b % 2][:], bank[4 + b % 4][:], ACT.Copy).then_inc(out_copied, 1)

            for b in range(B):
                td_copy(b)
                if b < B - 1:
                    out_copy(b)
            out_copy(B - 1)

        @block.vector
        def _(dve):
            def low(dst, src, hi):
                return dve.tensor_tensor(dst, src, hi.bitcast(F32), ALU.subtract)

            def split_lo(name):
                raw, hi, lo = split_views(name)
                dve.wait_ge(w12_hi, nth[name])
                if name == "b2":
                    dve.wait_ge(masks_ready, 1)
                    dve.scalar_tensor_tensor(out=lo, in0=hi.bitcast(F32), scalar=lo_rows32[:, 0:1], in1=raw,
                                             op0=ALU.mult, op1=ALU.add).then_inc(w12_lo, 1)
                else:
                    low(lo, raw, hi).then_inc(w12_lo, 1)

            def x1_add(b):
                cols = slice(b * S, (b + 1) * S)
                dve.wait_ge(l0_tr, b + 1)
                dve.tensor_tensor(x_f[:, :, cols], bank[2 + b % 2][:].rearrange("p (c t) -> p c t", c=C),
                                  x_f[:, :, cols], ALU.add).then_inc(x1_sum, 1)

            def x1_low(b):
                cols = slice(b * S, (b + 1) * S)
                dve.wait_ge(x1_hi, b + 1)
                low(xb[:, 1, :, cols], x_f[:, :, cols], xb[:, 0, :, cols]).then_inc(x1_lo, 1)

            dve.memset(lo_rows32[0:64], 0.0)
            dve.memset(lo_rows32[64:128], -1.0)
            for q in range(4):
                last = dve.memset(lo_rows16[32 * q:32 * q + 32], -1.0 * (q % 2))
            last.then_inc(masks_ready, 1)
            for b in range(1, B):
                dve.wait_ge(w0_hi, b)
                low(w0_hl[b % W0_RING][:, 1], w0_raw[b % W0_RING][:, 0:KC],
                    w0_hl[b % W0_RING][:, 0]).then_inc(w0_lo, 1)
                if b >= 3:
                    x1_add(b - 3)
                if b >= 4:
                    x1_low(b - 4)
                if b == 6:
                    split_lo("aw1")
            steps = [0]

            def step(ins):
                steps[0] += 1
                ins.then_inc(router_step, 1)
                dve.wait_ge(router_step, steps[0])

            dve.wait_ge(lang_in, 16)
            dve.wait_ge(iota_ready, 1)
            step(dve.tensor_copy(lang_f[:], lang_i[:]))
            step(dve.tensor_tensor(lang_bias[:], iota_e[:].unsqueeze(1).to_broadcast([P, B, E]),
                                   lang_f[:].unsqueeze(2).to_broadcast([P, B, E]), ALU.is_equal))
            step(dve.tensor_scalar(lang_bias[:], lang_bias[:], LANG_BIAS, None, ALU.mult))
            x1_add(5)
            x1_low(4)
            x1_add(6)
            x1_low(5)
            x1_add(7)
            split_lo("w1_0")
            x1_low(6)
            x1_low(7)
            split_lo("w1_1")

            def router(h):
                bcast = [P, HB, E]
                for j in range(HB):
                    dve.wait_ge(l1_tm, HB * h + j + 1)
                    ins = dve.tensor_reduce(h_sum[h][:, j], bank[j][:, 0:2 * TM1].rearrange(
                        "p (k n) -> p n k", k=2), AX_X, ALU.add)
                step(ins)
                step(dve.tensor_tensor(logits[:], h_sum[h][:, :, ER:TM1], lang_bias[:, HB * h:HB * h + HB], ALU.add))
                for j in range(HB):
                    ins = dve.max(top_v[:, j], logits[:, j])
                step(ins)
                if h == 1:
                    dve.wait_ge(gap_exp, 1)
                dve.tensor_tensor(gap[:], top_v[:, :, 1], top_v[:, :, 0], ALU.subtract).then_inc(gap_ready, 1)
                for j in range(HB):
                    ins = dve.max_index(top_i[:, j], top_v[:, j], logits[:, j])
                step(ins)
                step(dve.tensor_copy(top_f[:], top_i[:, :, 0:2]))
                for k in range(2):
                    dve.tensor_tensor(eq[:, k], iota_e[:].unsqueeze(1).to_broadcast(bcast),
                                      top_f[:, :, k:k + 1].to_broadcast(bcast), ALU.is_equal)
                dve.wait_ge(gap_exp, h + 1)
                step(dve.tensor_scalar(gate_w[:, 0], gap_e[:], 1.0, None, ALU.add))
                step(dve.reciprocal(gate_w[:, 1], gate_w[:, 0]))
                step(dve.tensor_scalar(gate_w[:, 2], gate_w[:, 1], SCALING1, None, ALU.mult))
                step(dve.tensor_tensor(gate_w[:, 3], gate_w[:, 2], gap_e[:], ALU.mult))
                for k in range(2):
                    ins = dve.tensor_tensor(eq[:, k], eq[:, k],
                                            gate_w[:, 2 + k].unsqueeze(2).to_broadcast(bcast), ALU.mult)
                step(ins)
                step(dve.tensor_tensor(logits[:], eq[:, 0], eq[:, 1], ALU.add))
                dve.tensor_tensor(h_gated[h][:].rearrange("p j (e r) -> p j e r", e=E),
                                  h_sum[h][:, :, 0:ER].rearrange("p j (e r) -> p j e r", e=E),
                                  logits[:].unsqueeze(3).to_broadcast([P, HB, E, R]),
                                  ALU.mult).then_inc(h_gated_ready, 1)

            def hg_low(h):
                cols = slice(h * HT, (h + 1) * HT)
                dve.wait_ge(hg_hi, h + 1)
                low(hg_hl[:, 1, cols], bank[0][:], hg_hl[:, 0, cols]).then_inc(hg_lo, 1)

            def x_add(l, h, o):
                n = number(l, h, o)
                dst = x_f[:, o, h * HT:(h + 1) * HT]
                dve.wait_ge(main_done, n + 1)
                if l == 1:
                    ins = dve.tensor_tensor(dst, bank[4 + n % 4][:], dst, ALU.add)
                else:
                    ins = dve.scalar_tensor_tensor(out=dst, in0=bank[4 + n % 4][:], scalar=bias_sb[:, o:o + 1],
                                                   in1=dst, op0=ALU.add, op1=ALU.add)
                ins.then_inc(x_sum, 1)

            def x_low(l, h, o):
                cols = slice(h * HT, (h + 1) * HT)
                xs = xa if l == 1 else xb
                dve.wait_ge(x_hi, number(l, h, o) + 1)
                low(xs[:, 1, o, cols], x_f[:, o, cols], xs[:, 0, o, cols]).then_inc(x_lo, 1)

            router(0)
            for o in range(2, C):
                split_lo(f"w1_{o}")
            split_lo("b1")
            split_lo("a2")
            hg_low(0)

            def residual(l, h, between):
                for o in range(C + 1):
                    if o < C:
                        x_add(l, h, o)
                    if o > 0:
                        x_low(l, h, o - 1)
                        if between:
                            split_lo(between.pop(0))

            residual(1, 0, ["w2_0", "w2_1", "w2_2"])
            router(1)
            split_lo("w2_3")
            hg_low(1)
            split_lo("b2")
            residual(1, 1, [])
            dve.wait_ge(bias_in, 16)
            thin = [0, 0]

            def summed(thin_cols, dst, n):
                thin[0] += 1
                dve.tensor_reduce(dst, thin_cols, AX_X, ALU.add).then_inc(thin_sum, 1)
                dve.wait_ge(thin_sum, thin[0])

            def after_hi(ins):
                thin[1] += 1
                ins.then_inc(thin_hi, 1)
                dve.wait_ge(thin_hi, thin[1])

            def t2_split(h):
                dve.wait_ge(l2_tm, h + 1)
                if h == 1:
                    pass
                cols = bank[h][:, 0:HB * 2 * R2].rearrange("p (j k r) -> p j r k", j=HB, k=2)
                summed(cols, t23_f[h][:], 4)
                parts = t2_parts[h][:].rearrange("p j (d k) r -> p j d k r", k=2)
                for j in range(HB):
                    t = t23_f[h][:, j].unsqueeze(1).to_broadcast([P, 2, R2])
                    ins = dve.tensor_copy(parts[:, j, :, 0].bitcast(F32R), t)
                after_hi(ins)
                for j in range(HB):
                    t = t23_f[h][:, j].unsqueeze(1).to_broadcast([P, 2, R2])
                    ins = low(parts[:, j, :, 1], t, parts[:, j, :, 0])
                ins.then_inc(t2_ready, 1)

            def gate_up_lo(fc, slot, n):
                dve.wait_ge(wgu_hi, n)
                low(wgu_hl[slot][:, 1], wgu_raw[slot][:], wgu_hl[slot][:, 0]).then_inc(wgu_lo, 1)
                dve.wait_ge(bgu_hi, n)
                dve.scalar_tensor_tensor(out=bgu_st[slot][:], in0=bgu_st[slot][:].bitcast(F32),
                                         scalar=lo_rows16[:, 0:1], in1=bgu_raw[slot][:],
                                         op0=ALU.mult, op1=ALU.add).then_inc(bgu_ready, 1)

            t2_split(0)
            split_lo("agu")
            residual(2, 0, [])
            t2_split(1)
            gate_up_lo(0, 0, 1)
            gate_up_lo(1, 1, 2)
            residual(2, 1, [])

            def t3_split(h):
                dve.wait_ge(l3_tm, h + 1)
                cols = bank[h][:, 0:HB * 2 * RG].rearrange("p (j k r) -> p j r k", j=HB, k=2)
                summed(cols, t23_f[h][:], 4)
                if h == 0:
                    dve.wait_ge(t3_zeroed, 1)
                def views(j):
                    part = t3_parts[h][:, j, :, 64 * (j % 2):64 * (j % 2) + 64]
                    part = part.rearrange("p g (d k r) -> p g d k r", d=2, k=2)
                    t = t23_f[h][:, j].rearrange("p (g r) -> p g r", g=2).unsqueeze(2).to_broadcast([P, 2, 2, R])
                    return part[:, :, :, 0], part[:, :, :, 1], t
                for j in range(HB):
                    hi, _, t = views(j)
                    ins = dve.tensor_copy(hi.bitcast(F32R), t)
                after_hi(ins)
                for j in range(HB):
                    hi, lo, t = views(j)
                    ins = low(lo, t, hi)
                ins.then_inc(t3_ready, 1)

            def mul_and_low(fc, h):
                n = 2 * fc + h
                cols = slice(h * HT, (h + 1) * HT)
                dve.wait_ge(silu_done, n + 1)
                dve.wait_ge(up_done, n + 1)
                dve.tensor_tensor(act_f[h][:], bank[5 + 2 * h][:], act_f[h][:], ALU.mult).then_inc(act_mul, 1)
                dve.wait_ge(act_hi, n + 1)
                low(act_hl[:, fc, 1, cols], act_f[h][:], act_hl[:, fc, 0, cols]).then_inc(act_lo, 1)

            def down_lo(f):
                dve.wait_ge(wd_hi, f + 1)
                low(wd_hl[f][:, 1], wd_raw[f % WD_RING][:], wd_hl[f][:, 0]).then_inc(wd_lo, 1)

            t3_split(0)
            t3_split(1)
            for h in range(H):
                mul_and_low(0, h)
            with dve.Fori(0, 4) as i:
                for u in range(2):
                    fc = 2 * i + 1 + u
                    gate_up_lo(fc + 1, u, fc + 2)
                    for h in range(H):
                        mul_and_low(fc, h)
            dve.wait_ge(ad_hi, 1)
            low(ad_hl[:, :, :, 1], ad_raw[:], ad_hl[:, :, :, 0]).then_inc(ad_lo, 1)
            gate_up_lo(FC - 1, 0, FC)
            for fc in (FC - 2, FC - 1):
                down_lo(fc - (FC - 2))
                for h in range(H):
                    mul_and_low(fc, h)
            for f in range(2, FC):
                down_lo(f)
            dve.wait_ge(bd_hi, 1)
            dve.scalar_tensor_tensor(out=bd_st[:], in0=bd_st[:].bitcast(F32), scalar=lo_rows16[:, 0:1],
                                     in1=bd_raw[:], op0=ALU.mult, op1=ALU.add).then_inc(bd_ready, 1)
            dve.wait_ge(td_zeroed, 1)
            for b in range(B):
                dve.wait_ge(td_done, b + 1)
                cols = bank[b % 2][:, 0:2 * R].rearrange("p (k r) -> p r k", k=2)
                dve.tensor_reduce(td_f[b % 2][:], cols, AX_X, ALU.add).then_inc(td_sum, 1)
                part = td_parts[b % 2][:, 64 * (b % 2):64 * (b % 2) + 64]
                part = part.rearrange("p (d k r) -> p d k r", d=2, k=2)
                t = td_f[b % 2][:].unsqueeze(1).to_broadcast([P, 2, R])
                dve.wait_ge(td_sum, b + 1)
                if b >= 2:
                    dve.wait_ge(td_tr, b - 1)
                dve.tensor_copy(part[:, :, 0].bitcast(F32R), t).then_inc(td_hi, 1)
                dve.wait_ge(td_hi, b + 1)
                low(part[:, :, 1], t, part[:, :, 0]).then_inc(td_ready, 1)

        @block.tensor
        def _(pe):
            def transposes(dst, srcs):
                for k, src in enumerate(srcs):
                    ins = pe.transpose(dst[:, k * P:(k + 1) * P], src, ident[:])
                return ins

            def transpose_y0(b):
                pe.wait_ge(y0_copied, b + 1)
                if b >= 2:
                    pe.wait_ge(x1_sum, b - 1)
                transposes(bank[2 + b % 2], [y0[b % 2][:, c * P:(c + 1) * P] for c in range(C)]).then_inc(l0_tr, 1)

            for b in range(B):
                cols = slice(b * S, (b + 1) * S)
                raw = w0_raw[b % W0_RING]
                pe.wait_ge(x_in[b], 16)
                if b >= 2:
                    pe.wait_ge(y0_copied, b - 1)
                if b == 0:
                    for c in range(C):
                        pe.wait_ge(w0c_in[c], 16)
                        ins = pe.matmul(bank[0][:], x_f[:, c, cols], raw[:, c], start=(c == 0), stop=(c == C - 1))
                else:
                    pe.wait_ge(w0_in[b % W0_RING], w0_landed(b))
                    pe.matmul(bank[b % 2][:], x_f[:, RAWC, cols], raw[:, RAWC], start=True,
                              stop=False).then_inc(w0_raw_used, 1)
                    pe.wait_ge(x0_lo, b)
                    pe.wait_ge(w0_lo, b)
                    hl = w0_hl[b % W0_RING]
                    for c in range(KC):
                        pe.matmul(bank[b % 2][:], xa[:, 0, c, cols], hl[:, 0, c], start=False, stop=False)
                        pe.matmul(bank[b % 2][:], xa[:, 0, c, cols], hl[:, 1, c], start=False, stop=False)
                        ins = pe.matmul(bank[b % 2][:], xa[:, 1, c, cols], hl[:, 0, c], start=False,
                                        stop=(c == KC - 1))
                ins.then_inc(l0_tm, 1)
                if b == 1:
                    pe.wait_ge(ident_ready, 1)
                if b >= 1:
                    transpose_y0(b - 1)

            def thin1(h, j):
                b = HB * h + j
                cols = slice(b * S, (b + 1) * S)
                pe.wait_ge(x1_lo, b + 1)
                if h == 0 and j < 2:
                    pe.wait_ge(y0_copied, B - 1 + j)
                elif h == 0:
                    pe.wait_ge(x1_sum, B - 3 + j)
                else:
                    pe.wait_ge(h_gated_ready, 1)
                for c in range(C):
                    for k in range(2):
                        ins = pe.matmul(bank[j][:, 0:2 * TM1], xb[:, k, c, cols],
                                        aw1_hl[:, c].rearrange("p k n -> p (k n)"),
                                        start=(c == 0 and k == 0), stop=(c == C - 1 and k == 1))
                ins.then_inc(l1_tm, 1)

            pe.wait_ge(w12_lo, nth["aw1"])
            thin1(0, 0)
            transpose_y0(B - 1)

            def split_product(dst, w_hi, w_lo, x, h, start, stop):
                cols = slice(h * HT, (h + 1) * HT)
                pe.matmul(dst, w_hi, x[0][:, cols], start=start, stop=False)
                pe.matmul(dst, w_hi, x[1][:, cols], start=False, stop=False)
                return pe.matmul(dst, w_lo, x[0][:, cols], start=False, stop=stop)

            def base(l, h, o):
                n = number(l, h, o)
                x, hl = (xb, w1_hl) if l == 1 else (xa, w2_hl)
                if n >= 4:
                    pe.wait_ge(x_sum, n - 3)
                pe.wait_ge(w12_lo, nth[f"w{l}_{o}"])
                for c in range(C):
                    split_product(bank[4 + n % 4][:], hl[:, 0, o, c], hl[:, 1, o, c], (x[:, 0, c], x[:, 1, c]), h,
                                  c == 0, False)

            def lora1(h, o):
                n = number(1, h, o)
                cols = slice(o * P, (o + 1) * P)
                split_product(bank[4 + n % 4][:], b1_hl[:, 0, cols], b1_hl[:, 1, cols],
                              (hg_hl[:, 0], hg_hl[:, 1]), h, False, True).then_inc(main_done, 1)

            for h in range(H):
                for j in range(HB):
                    if (h, j) != (0, 0):
                        thin1(h, j)
                for o in range(3):
                    base(1, h, o)
                pe.wait_ge(h_gated_ready, h + 1)
                transposes(bank[0], [h_gated[h][:, j] for j in range(HB)]).then_inc(l1_tr, 1)
                pe.wait_ge(w12_lo, nth["b1"])
                base(1, h, 3)
                pe.wait_ge(hg_lo, h + 1)
                for o in range(C):
                    lora1(h, o)

            pe.wait_ge(w12_lo, nth["a2"])
            for h in range(H):
                pe.wait_ge(x_lo, number(1, h, C - 1) + 1)
                pe.wait_ge(h_gated_ready, 2)
                for j in range(HB):
                    b = HB * h + j
                    cols = slice(b * S, (b + 1) * S)
                    dst = bank[h][:, j * 2 * R2:(j + 1) * 2 * R2]
                    for c in range(C):
                        for k in range(2):
                            ins = pe.matmul(dst, xa[:, k, c, cols], a2_hl[:, b, c],
                                            start=(c == 0 and k == 0), stop=(c == C - 1 and k == 1))
                ins.then_inc(l2_tm, 1)
                for o in range(2):
                    base(2, h, o)
                pe.wait_ge(t2_ready, h + 1)
                transposes(bank[2 + h], [t2_parts[h][:, j] for j in range(HB)]).then_inc(l2_tr, 1)
                base(2, h, 2)
                pe.wait_ge(w12_lo, nth["b2"])
                pe.wait_ge(t2_copied, h + 1)
                for o in range(C):
                    if o == 3:
                        base(2, h, 3)
                    pe.matmul(bank[4 + number(2, h, o) % 4][:], b2_st[:, o * P:(o + 1) * P],
                              t2_st[:, h * HT:(h + 1) * HT], start=False, stop=True).then_inc(main_done, 1)

            def thin3(h):
                pe.wait_ge(x_lo, number(2, h, C - 1) + 1)
                for j in range(HB):
                    b = HB * h + j
                    cols = slice(b * S, (b + 1) * S)
                    dst = bank[h][:, j * 2 * RG:(j + 1) * 2 * RG]
                    for c in range(C):
                        for k in range(2):
                            ins = pe.matmul(dst, xb[:, k, c, cols], agu_hl[:, b, c],
                                            start=(c == 0 and k == 0), stop=(c == C - 1 and k == 1))
                ins.then_inc(l3_tm, 1)

            def transpose3(h):
                pe.wait_ge(t3_ready, h + 1)
                if h == 1:
                    pe.wait_ge(t3_copied, 1)
                for g in range(2):
                    ins = transposes(bank[2 + g], [t3_parts[h][:, j, g] for j in range(HB)])
                ins.then_inc(l3_tr, 1)

            def gate_up_main(g, h, slot):
                for c in range(C):
                    hl = wgu_hl[slot]
                    split_product(bank[4 + 2 * h + g][:], hl[:, 0, c, g], hl[:, 1, c, g],
                                  (xb[:, 0, c], xb[:, 1, c]), h, c == 0, False)

            def gate_up_lora(g, h, slot):
                for q in range(2):
                    pair = 2 * h + q
                    ins = pe.matmul(bank[4 + 2 * h + g][:, q * 2 * S:(q + 1) * 2 * S], bgu_st[slot][:, pair, g],
                                    t3_st[:, g, pair * 2 * S:(pair + 1) * 2 * S], start=False, stop=(q == 1))
                ins.then_inc(up_done if g else gate_done, 1)

            pe.wait_ge(w12_lo, nth["agu"])
            thin3(0)
            pe.wait_ge(wgu_lo, 1)
            pe.wait_ge(x_sum, number(2, 0, 0) + 1 + 5)
            gate_up_main(0, 0, 0)
            transpose3(0)
            gate_up_main(1, 0, 0)
            thin3(1)
            pe.wait_ge(bgu_ready, 1)
            pe.wait_ge(t3_copied, 1)
            for g in range(2):
                gate_up_lora(g, 0, 0)
            gate_up_main(0, 1, 0)
            transpose3(1)
            gate_up_main(1, 1, 0)
            pe.wait_ge(t3_copied, 2)
            for g in range(2):
                gate_up_lora(g, 1, 0)
            with pe.Fori(0, (FC - 1) // 2) as i:
                for u in range(2):
                    fc = 2 * i + 1 + u
                    slot = 1 - u
                    pe.wait_ge(wgu_lo, fc + 1)
                    pe.wait_ge(bgu_ready, fc + 1)
                    for h in range(H):
                        pe.wait_ge(silu_done, 2 * fc - 1 + h)
                        gate_up_main(0, h, slot)
                        gate_up_lora(0, h, slot)
                        pe.wait_ge(act_mul, 2 * fc - 1 + h)
                        gate_up_main(1, h, slot)
                        gate_up_lora(1, h, slot)

            def act_tile(b, f, k):
                return act_hl[:, f, k, b * S:(b + 1) * S]

            def rank_product(b, f, k):
                return pe.matmul(bank[b % 2][:, 0:2 * R], act_tile(b, f, k), ad_hl[:, b, f],
                                 start=(f == 0 and k == 0), stop=(f == FC - 1 and k == 1))

            def transpose_td(b):
                pe.wait_ge(td_ready, b + 1)
                if b >= 2:
                    pe.wait_ge(td_copied, b - 1)
                transposes(bank[2 + b % 2], [td_parts[b % 2][:]]).then_inc(td_tr, 1)

            def finish(b):
                if b == 0:
                    pe.wait_ge(bd_ready, 1)
                pe.wait_ge(td_copied, b + 1)
                pe.matmul(bank[4 + b % 4][:], td_st[b % 2][:], bd_st[:, b // 2], start=False,
                          stop=True).then_inc(down_done, 1)

            pe.wait_ge(ad_lo, 1)
            for b in range(B):
                dst = bank[4 + b % 4][:]
                last = b == B - 1
                pe.wait_ge(act_lo, 2 * FC - 1 + (b >= HB))
                pe.wait_ge(act_mul, 2 * FC)
                if b >= 4:
                    pe.wait_ge(out_copied, b - 3)
                for c in range(C):
                    pe.matmul(dst[:, c * P:(c + 1) * P], x_f[:, c, b * S:(b + 1) * S], ident[:],
                              start=(c == 0), stop=False, is_transpose=True)
                if b >= 2:
                    pe.wait_ge(td_sum, b - 1)
                if last:
                    for f in range(FC):
                        for k in range(2):
                            ins = rank_product(b, f, k)
                    ins.then_inc(td_done, 1)
                for f in range(FC):
                    if b == 0:
                        pe.wait_ge(wd_lo, f + 1)
                    pe.matmul(dst, act_tile(b, f, 0), wd_hl[f][:, 0], start=False, stop=False)
                    pe.matmul(dst, act_tile(b, f, 0), wd_hl[f][:, 1], start=False, stop=False)
                    if not last:
                        rank_product(b, f, 0)
                    pe.matmul(dst, act_tile(b, f, 1), wd_hl[f][:, 0], start=False, stop=False)
                    if not last:
                        ins = rank_product(b, f, 1)
                    if b >= 1 and f == 3:
                        transpose_td(b - 1)
                    if b >= 1 and f == 6:
                        finish(b - 1)
                    if last and f == 8:
                        transpose_td(b)
                if not last:
                    ins.then_inc(td_done, 1)
            finish(B - 1)


def kernel(**inputs):
    import numpy as np
    import concourse.bacc as bacc
    from concourse import mybir as mb
    from concourse.bass_utils import run_bass_kernel_spmd as run

    a = {k: np.asarray(v) for k, v in inputs.items()}

    def chunked(w):
        *lead, k, n = w.shape
        return np.moveaxis(w.reshape(*lead, k // P, P, n), -3, -2)

    def padded(w, axis):
        shape = list(w.shape)
        shape[axis] = FC * P
        z = np.zeros(shape, w.dtype)
        z[tuple(slice(0, n) for n in w.shape)] = w
        return z

    def stacked(w, copies):
        *lead, r, n = w.shape
        return np.broadcast_to(w[..., None, :, :], (*lead, copies, r, n)).reshape(*lead, copies * r, n)

    t = lambda w: np.swapaxes(w, -1, -2)
    w_sq = lambda w: chunked(t(w)).reshape(P, C, C, P).transpose(0, 2, 1, 3)
    gu = lambda g, u: np.stack([g, u], axis=-2)
    bg, bu = (padded(t(a[f"L3_cond_B_{n}"][0]), 2).reshape(16, R, FC, P) for n in ("gate", "up"))
    wg, wu = (chunked(padded(t(a[f"L3_cond_W_{n}"]), 1)).reshape(P, C, FC, P) for n in ("gate", "up"))
    arrays = {
        "xT": chunked(t(a["x"])),
        "ids0": a["itok_B_0_15"][None], "ids1": a["itok_B_0_7"], "ids2": a["itok_B_0_4"][None],
        "ids3": a["itok_B_2_6"][None],
        "w0": chunked(t(a["L0_cond_weight"])).reshape(16, P, C * D),
        "w1": w_sq(a["L1_cond_W"]),
        "aw1": chunked(np.concatenate([t(a["L1_cond_A"].reshape(ER, D)), t(a["L1_cond_Wr"])], axis=1)),
        "b1": np.swapaxes(a["L1_cond_B"], 1, 2).reshape(ER, D),
        "w2": w_sq(a["L2_cond_weight"]),
        "a2": chunked(a["L2_cond_lora_A"]),
        "b2": stacked(t(a["L2_cond_lora_B"]), 4),
        "bias2": a["L2_cond_bias"].reshape(C, P).T,
        "wgu": gu(wg, wu).transpose(2, 0, 1, 3, 4),
        "agu": chunked(np.concatenate([t(a["L3_cond_A_gate"][0]), t(a["L3_cond_A_up"][0])], axis=2)),
        "bgu": stacked(gu(bg, bu).transpose(0, 2, 1, 3, 4).reshape(16, FC, R, 2 * P), 4),
        "wd": chunked(padded(t(a["L3_cond_W_down"]), 0)),
        "ad": chunked(padded(t(a["L3_cond_A_down"][0]), 1)),
        "bd": stacked(t(a["L3_cond_B_down"][0]), 4),
    }
    nc = bacc.Bacc("TRN2", target_bir_lowering=False, num_devices=1, dynamic_dma_scratch_size=1024)
    feed, args = {}, []
    for name, v in arrays.items():
        v = np.ascontiguousarray(v)
        feed[f"in_{name}"] = v
        args.append(nc.dram_tensor(f"in_{name}", v.shape, mb.dt.from_np(v.dtype), kind="ExternalInput").ap())
    out = nc.dram_tensor("out_0", (B, S, D), mb.dt.float32, kind="ExternalOutput").ap()
    bass_four_residual_layers(nc, *args, out)
    return run(nc, [feed], core_ids=[0]).results[0]["out_0"]
```

```python
from contextlib import ExitStack

import concourse.bass as bass
from concourse import mybir

F32 = mybir.dt.float32
F32R = mybir.dt.float32r
I32 = mybir.dt.int32
U32 = mybir.dt.uint32
ALU = mybir.AluOpType
ACT = mybir.ActivationFunctionType
AX_X = mybir.AxisListType.X

P = 128
B, S, D = 8, 128, 512
C = D // P
T = B * S
H = 2
HB = B // H
HT = T // H
E, R = 8, 16
ER = E * R
TM1 = ER + E
R2 = 32
RG = 2 * R
FC = 11
LANG_BIAS = 5.0
SCALING1 = 2.0
SCALING = 0.5
BANK = 512
KC = C - 1
WARM_UP = 9
W0_RING = 3


def bass_four_residual_layers(nc, xT, ids0, ids1, ids2, ids3, w0, w1, aw1, b1, w2, a2, b2, bias2,
                              wgu, agu, sel, bgu, wd, ad, bd, out):
    ctx = ExitStack()
    with ctx:
        base = (nc.sbuf_base + 31) // 32 * 32

        def at(name, off, shape, dt=F32):
            return nc.alloc_sbuf_tensor_at(name, [P, *shape], dt, offset=base + off)

        KB = 1024
        o_xf, o_xb, o_act = 0, 16 * KB, 48 * KB
        o_xa = o_act
        o_w0 = o_act + 32 * KB
        o_w1 = o_act + 56 * KB
        o_w2 = o_act + 72 * KB
        o_wgu = 136 * KB
        o_raw = o_wgu + 16 * KB
        o_slot2 = o_raw + 16 * KB
        o_bst = o_slot2 + 8 * KB
        o_tp = o_bst + 8 * KB
        o_ad = o_tp + 8 * KB
        o_misc = o_ad + 11 * KB

        x_f = at("x_f", o_xf, [C, T])
        xa = at("xa", o_xa, [2, C, T], F32R)
        xb = at("xb", o_xb, [2, C, T], F32R)
        w0_raw = [at(f"w0_raw{i}", o_raw + i * 8 * KB, [C, D]) for i in range(W0_RING)]
        w0_hl = [at(f"w0_hl{i}", (o_w0, o_w0 + 12 * KB, o_w2)[i], [2, KC, D], F32R)
                 for i in range(W0_RING)]
        y0 = [at(f"y0_{i}", o_tp + i * 2 * KB, [D]) for i in range(2)]
        w1_hl = at("w1_hl", o_w1, [2, C, C, P], F32R)
        aw1_hl = at("aw1_hl", o_wgu, [C, 2, TM1], F32R)
        b1_hl = at("b1_hl", o_wgu + 5 * KB, [2, D], F32R)
        aw1_raw = at("aw1_raw", o_bst, [C, TM1])
        b1_raw = at("b1_raw", o_bst + 3 * KB, [D])
        h_sum = [at(f"h_sum{i}", o_wgu + (9 + i * 3) * KB, [HB, TM1]) for i in range(H)]
        h_gated = [at(f"h_gated{i}", o_w0 + 20 * KB + i * 2 * KB, [HB, ER]) for i in range(H)]
        hg_hl = at("hg_hl", o_w0 + 12 * KB, [2, T], F32R)
        w2_raw = at("w2_raw", o_raw, [C, C, P])
        w2_hl = at("w2_hl", o_w2, [2, C, C, P], F32R)
        a2_raw = at("a2_raw", o_tp + 4 * KB, [B, C, R2])
        a2_hl = at("a2_hl", o_ad, [B, C, 2, R2], F32R)
        b2_raw = at("b2_raw", o_bst + 5 * KB, [D])
        b2_hl = at("b2_hl", o_slot2, [2, D], F32R)
        t2_st = at("t2_st", o_w0 + 12 * KB, [T], F32R)
        sel_r = at("sel_r", o_slot2 + 4 * KB, [2, P], F32R)
        agu_raw = at("agu_raw", o_w0 + 8 * KB, [B, C, RG])
        agu_hl = at("agu_hl", o_w0, [B, C, 2, RG], F32R)
        t3_uv = at("t3_uv", o_w0 + 16 * KB, [T], F32R)
        t3_st = at("t3_st", o_tp, [2, T], F32R)
        bgu_raw = [at(f"bgu_raw{i}", o_raw + i * 4 * KB, [B // 2, 2, P]) for i in range(2)]
        wgu_raw = [at(f"wgu_raw{i}", o_raw + (8 + i * 4) * KB, [C, 2, P]) for i in range(2)]
        bgu_st = [at(f"bgu_st{i}", o_bst + i * 4 * KB, [B // 2, 2, P], F32R) for i in range(2)]
        wgu_hl = [at(f"wgu_hl{i}", o_wgu + i * 8 * KB, [2, C, 2, P], F32R) for i in range(2)]
        act_hl = at("act_hl", o_act, [FC, 2, T], F32R)
        act_f = [at(f"act_f{i}", o_slot2 + i * 2 * KB, [HT]) for i in range(2)]
        ad_raw = at("ad_raw", o_act + 80 * KB, [B, FC, R])
        ad_hl = at("ad_hl", o_ad, [B, FC, 2, R], F32R)
        td_st = at("td_st", o_slot2 + 4 * KB, [T], F32R)
        td_odd = [at(f"td_odd{i}", o_slot2 + i * KB, [HB // 2, S], F32R) for i in range(H)]
        bd_raw = at("bd_raw", o_raw, [B // 2, D])
        bd_hl = at("bd_hl", o_bst, [2, B // 2, D], F32R)
        m = [o_misc]

        def own(name, shape, dt=F32):
            n = 4
            for k in shape:
                n *= k
            t = at(name, m[0], shape, dt)
            m[0] += (n + 31) // 32 * 32
            return t

        ident = own("ident", [P])
        wd_own = own("wd_own", [FC, P])
        wd_raw = [wd_own, at("wd_raw1", o_raw + 8 * KB, [FC, P]), wd_own, at("wd_raw3", o_xb + 22 * KB, [FC, P])]
        w1_raw = at("w1_raw", m[0], [C, C, P])
        wd_hl = [own("wd_hl0", [2, FC, P], F32R), at("wd_hl1", o_xb, [2, FC, P], F32R),
                 at("wd_hl2", o_xb + 11 * KB, [2, FC, P], F32R), at("wd_hl3", o_wgu, [2, FC, P], F32R)]
        sel_raw = own("sel_raw", [2 * P + 1])
        bias_sb = own("bias_sb", [C])
        lo_rows16 = own("lo_rows16", [1])
        lang_i = own("lang_i", [B], I32)
        lang_f = own("lang_f", [B])
        iota_e = own("iota_e", [E])
        lang_bias = own("lang_bias", [B, E])
        logits = own("logits", [HB, E])
        top_v = own("top_v", [HB, 8])
        top_i = own("top_i", [HB, 8], U32)
        top_f = own("top_f", [HB, 2])
        gap = own("gap", [HB])
        gap_e = own("gap_e", [HB])
        gate_w = own("gate_w", [4, HB])
        eq = own("eq", [2, HB, E])
        assert base + m[0] <= nc.sbuf_usable_end, (base + m[0], nc.sbuf_usable_end)

        bank = [ctx.enter_context(nc.psum_tensor(f"bank{i}", [P, BANK], F32)) for i in range(8)]

        def sem(name):
            return ctx.enter_context(nc.semaphore(name))

        x_in = [sem(f"x_in{b}") for b in range(B)]
        w0c_in = [sem(f"w0c_in{c}") for c in range(C)]
        w0_in = [[sem(f"w0_in{i}_{k}") for k in range(KC)] for i in range(W0_RING)]
        aw1_in, b1_in, lang_in = sem("aw1_in"), sem("b1_in"), sem("lang_in")
        w1_in = [sem(f"w1_in{o}") for o in range(C)]
        w2_in, a2_in, b2_in, bias_in = sem("w2_in"), sem("a2_in"), sem("b2_in"), sem("bias_in")
        agu_in, sel_in = sem("agu_in"), sem("sel_in")
        wgu_in = [sem(f"wgu_in{i}") for i in range(2)]
        bgu_in = [sem(f"bgu_in{i}") for i in range(2)]
        ad_in, bd_in = sem("ad_in"), sem("bd_in")
        wd_in = [sem(f"wd_in{o}") for o in range(C)]
        out_sent = sem("out_sent")
        const_step, ident_ready, masks_ready, iota_ready = (sem(n) for n in (
            "const_step", "ident_ready", "masks_ready", "iota_ready"))
        t3_zeroed, td_zeroed = sem("t3_zeroed"), sem("td_zeroed")
        x0_hi, x0_lo = sem("x0_hi"), sem("x0_lo")
        w0_raw_used, l0_tm, l0_tr = sem("w0_raw_used"), sem("l0_tm"), sem("l0_tr")
        l1_tm, l1_tr = sem("l1_tm"), sem("l1_tr")
        l2_tm, l3_tm, t3_done = sem("l2_tm"), sem("l3_tm"), sem("t3_done")
        main_done = sem("main_done")
        gate_done, up_done = sem("gate_done"), sem("up_done")
        td_done, down_done = sem("td_done"), sem("down_done")
        w0_hi, y0_copied, x1_hi = sem("w0_hi"), sem("y0_copied"), sem("x1_hi")
        w12_hi, gap_exp, hg_hi = sem("w12_hi"), sem("gap_exp"), sem("hg_hi")
        x_hi, t2_hi, t3_uv_hi, t3_hi = sem("x_hi"), sem("t2_hi"), sem("t3_uv_hi"), sem("t3_hi")
        sel_copied = sem("sel_copied")
        wgu_hi, bgu_hi, silu_done, act_hi = sem("wgu_hi"), sem("bgu_hi"), sem("silu_done"), sem("act_hi")
        ad_hi, down_hi, td_hi = sem("ad_hi"), sem("down_hi"), sem("td_hi")
        w0_lo, x1_sum, x1_lo = sem("w0_lo"), sem("x1_sum"), sem("x1_lo")
        ranks_summed = sem("ranks_summed")
        w12_lo, router_step, gap_ready, h_gated_ready = (sem(n) for n in (
            "w12_lo", "router_step", "gap_ready", "h_gated_ready"))
        hg_lo, x_sum, x_lo = sem("hg_lo"), sem("x_sum"), sem("x_lo")
        t2_lo, t3_uv_lo, t3_lo = sem("t2_lo"), sem("t3_uv_lo"), sem("t3_lo")
        wgu_lo, bgu_ready, act_mul, act_lo = sem("wgu_lo"), sem("bgu_ready"), sem("act_mul"), sem("act_lo")
        ad_lo, down_lo, td_lo, x3_sum = sem("ad_lo"), sem("down_lo"), sem("td_lo"), sem("x3_sum")

        def w0_landed(b):
            return 16 * (b // W0_RING + (b % W0_RING > 0))

        def number(l, h, o):
            return 8 * (l - 1) + C * h + o

        def thin1_bank(h, j):
            return bank[4 + j if h == 0 else j]

        splits = ["aw1"] + [f"w1_{o}" for o in range(C)] + ["b1", "a2"] + [f"w2_{o}" for o in range(C)] + ["b2", "agu"]
        nth = {name: i + 1 for i, name in enumerate(splits)}

        def split_views(name):
            if name == "aw1":
                return aw1_raw[:], aw1_hl[:, :, 0], aw1_hl[:, :, 1]
            if name == "b1":
                return b1_raw[:], b1_hl[:, 0], b1_hl[:, 1]
            if name == "a2":
                return a2_raw[:], a2_hl[:, :, :, 0], a2_hl[:, :, :, 1]
            if name == "agu":
                return agu_raw[:], agu_hl[:, :, :, 0], agu_hl[:, :, :, 1]
            if name == "b2":
                return b2_raw[:], b2_hl[:, 0], b2_hl[:, 1]
            raw, hl = (w1_raw, w1_hl) if name[1] == "1" else (w2_raw, w2_hl)
            o = int(name[3:])
            return raw[:, o], hl[:, 0, o], hl[:, 1, o]

        split_source = {"aw1": (aw1_in, 16), "b1": (b1_in, 16), "a2": (a2_in, 16 * B), "agu": (agu_in, 16 * B),
                        "b2": (b2_in, 16)}
        for o in range(C):
            split_source[f"w1_{o}"] = (w1_in[o], 16)
            split_source[f"w2_{o}"] = (w2_in, 16)

        T3_BLOCKS = [(g, par) for g in range(2) for par in range(2)]

        def t3_block(h, g, par):
            rows = slice(64 * par, 64 * par + 64)
            dst = t3_st[rows, g, h * HT:(h + 1) * HT].rearrange("p (q b s) -> p q b s", b=2, s=S)
            src = bank[2 + g][rows].rearrange("p (q b s) -> p q b s", b=2, s=S)
            return dst[:, :, par], src[:, :, par]

        down_splits = {
            "wd_0": (wd_in[0], 16, wd_raw[0], wd_hl[0]), "wd_1": (wd_in[1], 16, wd_raw[1], wd_hl[1]),
            "bd": (bd_in, 16 * B, bd_raw, bd_hl),
            "wd_2": (wd_in[2], 16, wd_raw[2], wd_hl[2]), "wd_3": (wd_in[3], 16, wd_raw[3], wd_hl[3])}
        down_nth = {name: i + 1 for i, name in enumerate(down_splits)}

        def td_block(h, par):
            def of_parity(t):
                return t.rearrange("p (q b s) -> p q b s", b=2, s=S)[:, :, par]

            cols = slice(h * HT, (h + 1) * HT)
            first = 64 * par
            return (of_parity(bank[h][0:2 * R]), of_parity(td_st[first:first + 2 * R, cols]),
                    of_parity(td_st[first + 2 * R:first + 4 * R, cols]))

        block = ctx.enter_context(nc.Block())

        @block.sync
        def _(sp):
            def id_of(src, b, last):
                return sp.value_load(src[0:1, b:b + 1], min_val=0, max_val=last)

            for b in range(2):
                sp.dma_start(x_f[:, :, b * S:(b + 1) * S], xT[b]).then_inc(x_in[b], 16)
            adapter = id_of(ids0, 0, w0.shape[0] - 1)
            for c in range(C):
                sp.dma_start(w0_raw[0][:, c], w0[adapter][:, c * D:(c + 1) * D]).then_inc(w0c_in[c], 16)
            for b in range(1, B):
                adapter = id_of(ids0, b, w0.shape[0] - 1)
                if b >= 2:
                    sp.dma_start(x_f[:, :, b * S:(b + 1) * S], xT[b]).then_inc(x_in[b], 16)
                if b == W0_RING:
                    sp.wait_ge(l0_tm, 1)
                if b > W0_RING:
                    sp.wait_ge(w0_raw_used, b - W0_RING)
                    sp.wait_ge(w0_lo, KC * (b - W0_RING))
                for k, (first, end) in enumerate(((0, 2), (2, 3), (3, 4))):
                    sp.dma_start(w0_raw[b % W0_RING][:, first:end],
                                 w0[adapter][:, first * D:end * D]).then_inc(w0_in[b % W0_RING][k], 16)
                if b == 2:
                    sp.dma_start(aw1_raw[:], aw1).then_inc(aw1_in, 16)
                    sp.dma_start(lang_i[:], ids1.partition_broadcast(P)).then_inc(lang_in, 16)
            for o in range(C):
                sp.dma_start(w1_raw[:, o], w1[:, o]).then_inc(w1_in[o], 16)
            sp.dma_start(b1_raw[:], b1).then_inc(b1_in, 16)
            sp.wait_ge(w0_raw_used, 6)
            sp.wait_ge(w0_lo, KC * 6)
            sp.dma_start(w2_raw[:], w2).then_inc(w2_in, 16)
            for b in range(B):
                sp.dma_start(a2_raw[:, b], a2[id_of(ids2, b, a2.shape[0] - 1)]).then_inc(a2_in, 16)
            sp.dma_start(b2_raw[:], b2).then_inc(b2_in, 16)
            sp.dma_start(bias_sb[:], bias2).then_inc(bias_in, 16)
            sp.dma_start(sel_raw[:], sel).then_inc(sel_in, 16)
            adapter3 = [id_of(ids3, b, agu.shape[0] - 1) for b in range(B)]
            sp.wait_ge(l0_tm, 8)
            for b in range(B):
                sp.dma_start(agu_raw[:, b], agu[adapter3[b]]).then_inc(agu_in, 16)

            def load_gate_up(fc, slot):
                sp.dma_start(wgu_raw[slot][:], wgu[fc]).then_inc(wgu_in[slot], 16)
                for b in range(B):
                    rows = slice(64 * (b % 2), 64 * (b % 2) + 64)
                    sp.dma_start(bgu_raw[slot][rows, b // 2], bgu[adapter3[b], fc]).then_inc(bgu_in[slot], 16)

            sp.wait_ge(w12_lo, nth["w2_3"])
            load_gate_up(0, 0)
            load_gate_up(1, 1)
            with sp.Fori(0, 4) as i:
                for u in range(2):
                    fc = 2 * i + 2 + u
                    sp.wait_ge(wgu_lo, 2 * i + 1 + u)
                    sp.wait_ge(bgu_ready, 2 * i + 1 + u)
                    load_gate_up(fc, u)
            sp.wait_ge(wgu_lo, FC - 2)
            sp.wait_ge(bgu_ready, FC - 2)
            load_gate_up(FC - 1, 0)
            for b in range(B):
                sp.dma_start(ad_raw[:, b], ad[adapter3[b]]).then_inc(ad_in, 16)
            sp.dma_start(wd_raw[0][:], wd[0]).then_inc(wd_in[0], 16)
            sp.wait_ge(wgu_lo, FC)
            sp.wait_ge(bgu_ready, FC)
            sp.dma_start(wd_raw[1][:], wd[1]).then_inc(wd_in[1], 16)
            for b in range(B):
                rows = slice(64 * (b % 2), 64 * (b % 2) + 64)
                sp.dma_start(bd_raw[rows, b // 2], bd[adapter3[b]]).then_inc(bd_in, 16)
            sp.wait_ge(down_lo, down_nth["wd_0"])
            sp.dma_start(wd_raw[2][:], wd[2]).then_inc(wd_in[2], 16)
            sp.wait_ge(up_done, 2 * FC)
            sp.dma_start(wd_raw[3][:], wd[3]).then_inc(wd_in[3], 16)
            for h in range(H):
                for o in range(C):
                    sp.wait_ge(x3_sum, C * h + o + 1)
                    cols = slice(h * HT, (h + 1) * HT)
                    sp.dma_start(out[o, :, cols], x_f[:, o, cols]).then_inc(out_sent, 16)
            sp.wait_ge(out_sent, 16 * H * C)

        @block.gpsimd
        def _(pool):
            pool.memset(ident[:], 0.0).then_inc(const_step, 1)
            pool.wait_ge(const_step, 1)
            pool.affine_select(out=ident[:], in_=ident[:], compare_op=ALU.not_equal, fill=1.0, base=0,
                               pattern=[[-1, P]], channel_multiplier=1).then_inc(ident_ready, 1)
            pool.iota(iota_e[:], [[1, E]], base=0, channel_multiplier=0,
                      allow_small_or_imprecise_dtypes=True).then_inc(iota_ready, 1)
            for b in range(1, B):
                cols = slice(b * S, (b + 1) * S)
                pool.wait_ge(x_in[b], 16)
                pool.tensor_copy(xa[:, 0, 1:C, cols], x_f[:, 1:C, cols]).then_inc(x0_hi, 1)
                pool.wait_ge(x0_hi, b)
                pool.tensor_tensor(xa[:, 1, 1:C, cols], x_f[:, 1:C, cols],
                                   xa[:, 0, 1:C, cols].bitcast(F32), ALU.subtract).then_inc(x0_lo, 1)
            pool.wait_ge(l0_tr, B)
            pool.wait_ge(w12_lo, nth["a2"])
            pool.memset(t3_st[:].bitcast(F32), 0.0).then_inc(t3_zeroed, 1)
            pool.wait_ge(t3_done, 2)
            pool.memset(td_st[:].bitcast(F32), 0.0).then_inc(td_zeroed, 1)

        @block.scalar
        def _(act):
            def high(dst, src):
                return act.activation(dst, src, ACT.Copy)

            def split_hi(name):
                s, n = split_source[name]
                act.wait_ge(s, n)
                raw, hi, _ = split_views(name)
                high(hi, raw).then_inc(w12_hi, 1)

            def copy_y0(b):
                act.wait_ge(l0_tm, b + 1)
                if b >= 2:
                    act.wait_ge(l0_tr, b - 1)
                act.activation(y0[b % 2][:], bank[b % 2][:], ACT.Copy).then_inc(y0_copied, 1)

            def x1_high(b):
                cols = slice(b * S, (b + 1) * S)
                act.wait_ge(x1_sum, b + 1)
                high(xb[:, 0, :, cols], x_f[:, :, cols]).then_inc(x1_hi, 1)

            for b in range(1, B):
                if b > W0_RING:
                    act.wait_ge(l0_tm, b - W0_RING + 1)
                if b == 3:
                    split_hi("aw1")
                for k in range(KC):
                    if k == KC - 1:
                        copy_y0(b - 1)
                    act.wait_ge(w0_in[b % W0_RING][k], w0_landed(b))
                    high(w0_hl[b % W0_RING][:, 0, k], w0_raw[b % W0_RING][:, 1 + k]).then_inc(w0_hi, 1)
                if b == 7:
                    split_hi("w1_0")
                    split_hi("w1_1")
                if b >= 2:
                    x1_high(b - 2)
            split_hi("w1_2")
            copy_y0(7)
            x1_high(6)
            split_hi("w1_3")
            split_hi("b1")

            def router_exp(h):
                act.wait_ge(gap_ready, h + 1)
                act.activation(gap_e[:], gap[:], ACT.Exp).then_inc(gap_exp, 1)

            def hg_high(h):
                act.wait_ge(l1_tr, h + 1)
                high(hg_hl[:, 0, h * HT:(h + 1) * HT], bank[0][:]).then_inc(hg_hi, 1)

            def x_high(l, h, o):
                n = number(l, h, o)
                dst = (xa if l == 1 else xb)[:, 0, o, h * HT:(h + 1) * HT]
                act.wait_ge(x_sum, n + 1)
                high(dst, x_f[:, o, h * HT:(h + 1) * HT]).then_inc(x_hi, 1)

            router_exp(0)
            x1_high(7)
            hg_high(0)
            split_hi("a2")
            for o in range(C):
                x_high(1, 0, o)
                split_hi(f"w2_{o}")
            router_exp(1)
            hg_high(1)
            split_hi("b2")
            for o in range(C):
                x_high(1, 1, o)

            def t2_high(h):
                act.wait_ge(l2_tm, h + 1)
                act.activation(t2_st[0:2 * R2, h * HT:(h + 1) * HT], bank[h][0:2 * R2], ACT.Copy,
                               scale=SCALING).then_inc(t2_hi, 1)

            def gate_up_hi(fc, slot, uses, free):
                act.wait_ge(wgu_in[slot], 16 * uses)
                if free is not None:
                    act.wait_ge(up_done, free)
                high(wgu_hl[slot][:, 0], wgu_raw[slot][:]).then_inc(wgu_hi, 1)
                act.wait_ge(bgu_in[slot], 16 * B * uses)
                high(bgu_st[slot][:], bgu_raw[slot][:]).then_inc(bgu_hi, 1)

            t2_high(0)
            split_hi("agu")
            act.wait_ge(sel_in, 16)
            high(sel_r[:], sel_raw[:, 0:2 * P].rearrange("p (g m) -> p g m", g=2)).then_inc(sel_copied, 1)
            for o in range(C):
                x_high(2, 0, o)
            t2_high(1)
            gate_up_hi(0, 0, 1, None)
            gate_up_hi(1, 1, 1, None)
            for o in range(C):
                x_high(2, 1, o)

            def t3_uv_high(h):
                act.wait_ge(l3_tm, h + 1)
                high(t3_uv[0:2 * RG, h * HT:(h + 1) * HT], bank[h][0:2 * RG]).then_inc(t3_uv_hi, 1)

            def t3_high(h):
                act.wait_ge(t3_done, h + 1)
                act.wait_ge(t3_zeroed, 1)
                for g, par in T3_BLOCKS:
                    dst, src = t3_block(h, g, par)
                    high(dst, src).then_inc(t3_hi, 1)

            def silu_and_high(fc, h):
                n = 2 * fc + h
                act.wait_ge(gate_done, n + 1)
                act.activation(act_f[h][:], bank[4 + 2 * h][:], ACT.Silu).then_inc(silu_done, 1)
                act.wait_ge(act_mul, n + 1)
                high(act_hl[:, fc, 0, h * HT:(h + 1) * HT], act_f[h][:]).then_inc(act_hi, 1)

            def down_split_hi(name):
                s, n, raw, hl = down_splits[name]
                act.wait_ge(s, n)
                high(hl[:, 0], raw[:]).then_inc(down_hi, 1)

            def td_high(h):
                act.wait_ge(td_done, h + 1)
                act.wait_ge(td_zeroed, 1)
                for par in range(2):
                    src, dst, _ = td_block(h, par)
                    act.activation(dst, src, ACT.Copy, scale=SCALING).then_inc(td_hi, 1)
                act.activation(td_odd[h][0:2 * R], src, ACT.Copy, scale=SCALING).then_inc(td_hi, 1)

            t3_uv_high(0)
            t3_high(0)
            t3_uv_high(1)
            silu_and_high(0, 0)
            t3_high(1)
            silu_and_high(0, 1)
            with act.Fori(0, 4) as i:
                for u in range(2):
                    fc = 2 * i + 1 + u
                    gate_up_hi(fc + 1, u, i + 2 if u == 0 else i + 2, 4 * i + 2 + 2 * u)
                    for h in range(H):
                        if h == 0:
                            act.wait_ge(act_lo, 2 * fc - 1)
                        else:
                            act.wait_ge(act_lo, 2 * fc)
                        silu_and_high(fc, h)
            act.wait_ge(ad_in, 16 * B)
            high(ad_hl[:, :, :, 0], ad_raw[:]).then_inc(ad_hi, 1)
            gate_up_hi(FC - 1, 0, 6, 2 * (FC - 2))
            down_split_hi("wd_0")
            for fc in (FC - 2, FC - 1):
                for h in range(H):
                    act.wait_ge(act_lo, 2 * fc - 1 + h)
                    silu_and_high(fc, h)
            act.wait_ge(up_done, 2 * FC)
            down_split_hi("wd_1")
            down_split_hi("bd")
            act.wait_ge(act_lo, 2 * FC)
            td_high(0)
            down_split_hi("wd_2")
            down_split_hi("wd_3")
            td_high(1)

        @block.vector
        def _(dve):
            def low(dst, src, hi):
                return dve.tensor_tensor(dst, src, hi.bitcast(F32), ALU.subtract)

            def split_lo(name):
                raw, hi, lo = split_views(name)
                dve.wait_ge(w12_hi, nth[name])
                low(lo, raw, hi).then_inc(w12_lo, 1)

            def x1_add(b):
                cols = slice(b * S, (b + 1) * S)
                dve.wait_ge(l0_tr, b + 1)
                dve.tensor_tensor(x_f[:, :, cols], bank[2 + b % 2][:].rearrange("p (c t) -> p c t", c=C),
                                  x_f[:, :, cols], ALU.add).then_inc(x1_sum, 1)

            def x1_low(b):
                cols = slice(b * S, (b + 1) * S)
                dve.wait_ge(x1_hi, b + 1)
                low(xb[:, 1, :, cols], x_f[:, :, cols], xb[:, 0, :, cols]).then_inc(x1_lo, 1)

            def sum_ranks1(h, j):
                dve.wait_ge(l1_tm, HB * h + j + 1)
                dve.tensor_reduce(h_sum[h][:, j], thin1_bank(h, j)[:, 0:2 * TM1].rearrange(
                    "p (k n) -> p n k", k=2), AX_X, ALU.add).then_inc(ranks_summed, 1)

            steps = [0]

            def step(ins):
                steps[0] += 1
                ins.then_inc(router_step, 1)
                dve.wait_ge(router_step, steps[0])

            def bias_of_language():
                dve.wait_ge(lang_in, 16)
                dve.wait_ge(iota_ready, 1)
                step(dve.tensor_copy(lang_f[:], lang_i[:]))
                step(dve.tensor_tensor(lang_bias[:], iota_e[:].unsqueeze(1).to_broadcast([P, B, E]),
                                       lang_f[:].unsqueeze(2).to_broadcast([P, B, E]), ALU.is_equal))
                step(dve.tensor_scalar(lang_bias[:], lang_bias[:], LANG_BIAS, None, ALU.mult))

            for q in range(4):
                last = dve.memset(lo_rows16[32 * q:32 * q + 32], -1.0 * (q % 2))
            last.then_inc(masks_ready, 1)
            for b in range(1, B):
                if b == 3:
                    split_lo("aw1")
                for k in range(KC):
                    dve.wait_ge(w0_hi, KC * (b - 1) + k + 1)
                    low(w0_hl[b % W0_RING][:, 1, k], w0_raw[b % W0_RING][:, 1 + k],
                        w0_hl[b % W0_RING][:, 0, k]).then_inc(w0_lo, 1)
                if b == 7:
                    split_lo("w1_0")
                    split_lo("w1_1")
                x1_add(b - 1)
                if b >= 2:
                    x1_low(b - 2)
                if b == 4:
                    bias_of_language()
                if b >= 5:
                    sum_ranks1(0, b - 5)
            split_lo("w1_2")
            sum_ranks1(0, 3)

            def router(h):
                bcast = [P, HB, E]
                if h == 1:
                    for j in range(HB):
                        sum_ranks1(1, j)
                dve.wait_ge(ranks_summed, HB * h + HB)
                step(dve.tensor_tensor(logits[:], h_sum[h][:, :, ER:TM1], lang_bias[:, HB * h:HB * h + HB], ALU.add))
                for j in range(HB):
                    ins = dve.max(top_v[:, j], logits[:, j])
                step(ins)
                if h == 1:
                    dve.wait_ge(gap_exp, 1)
                dve.tensor_tensor(gap[:], top_v[:, :, 1], top_v[:, :, 0], ALU.subtract).then_inc(gap_ready, 1)
                for j in range(HB):
                    ins = dve.max_index(top_i[:, j], top_v[:, j], logits[:, j])
                step(ins)
                step(dve.tensor_copy(top_f[:], top_i[:, :, 0:2]))
                for k in range(2):
                    dve.tensor_tensor(eq[:, k], iota_e[:].unsqueeze(1).to_broadcast(bcast),
                                      top_f[:, :, k:k + 1].to_broadcast(bcast), ALU.is_equal)
                dve.wait_ge(gap_exp, h + 1)
                step(dve.tensor_scalar(gate_w[:, 0], gap_e[:], 1.0, None, ALU.add))
                step(dve.reciprocal(gate_w[:, 1], gate_w[:, 0]))
                step(dve.tensor_scalar(gate_w[:, 2], gate_w[:, 1], SCALING1, None, ALU.mult))
                step(dve.tensor_tensor(gate_w[:, 3], gate_w[:, 2], gap_e[:], ALU.mult))
                for k in range(2):
                    ins = dve.tensor_tensor(eq[:, k], eq[:, k],
                                            gate_w[:, 2 + k].unsqueeze(2).to_broadcast(bcast), ALU.mult)
                step(ins)
                step(dve.tensor_tensor(logits[:], eq[:, 0], eq[:, 1], ALU.add))
                dve.tensor_tensor(h_gated[h][:].rearrange("p j (e r) -> p j e r", e=E),
                                  h_sum[h][:, :, 0:ER].rearrange("p j (e r) -> p j e r", e=E),
                                  logits[:].unsqueeze(3).to_broadcast([P, HB, E, R]),
                                  ALU.mult).then_inc(h_gated_ready, 1)

            def hg_low(h):
                cols = slice(h * HT, (h + 1) * HT)
                dve.wait_ge(hg_hi, h + 1)
                low(hg_hl[:, 1, cols], bank[0][:], hg_hl[:, 0, cols]).then_inc(hg_lo, 1)

            def x_add(l, h, o):
                n = number(l, h, o)
                dst = x_f[:, o, h * HT:(h + 1) * HT]
                dve.wait_ge(main_done, n + 1)
                if l == 1:
                    ins = dve.tensor_tensor(dst, bank[4 + n % 4][:], dst, ALU.add)
                else:
                    ins = dve.scalar_tensor_tensor(out=dst, in0=bank[4 + n % 4][:], scalar=bias_sb[:, o:o + 1],
                                                   in1=dst, op0=ALU.add, op1=ALU.add)
                ins.then_inc(x_sum, 1)

            def x_low(l, h, o):
                cols = slice(h * HT, (h + 1) * HT)
                xs = xa if l == 1 else xb
                dve.wait_ge(x_hi, number(l, h, o) + 1)
                low(xs[:, 1, o, cols], x_f[:, o, cols], xs[:, 0, o, cols]).then_inc(x_lo, 1)

            router(0)
            split_lo("w1_3")
            x1_add(7)
            x1_low(6)
            x1_low(7)
            split_lo("b1")
            hg_low(0)
            split_lo("a2")

            def residual(l, h, between):
                for o in range(C + 1):
                    if o < C:
                        x_add(l, h, o)
                    if o > 0:
                        x_low(l, h, o - 1)
                        if between:
                            split_lo(between.pop(0))

            residual(1, 0, ["w2_0", "w2_1", "w2_2"])
            router(1)
            split_lo("w2_3")
            hg_low(1)
            split_lo("b2")
            residual(1, 1, [])
            dve.wait_ge(bias_in, 16)

            def t2_low(h):
                cols = slice(h * HT, (h + 1) * HT)
                dve.wait_ge(t2_hi, h + 1)
                dve.scalar_tensor_tensor(out=t2_st[2 * R2:4 * R2, cols], in0=bank[h][0:2 * R2], scalar=SCALING,
                                         in1=t2_st[0:2 * R2, cols].bitcast(F32), op0=ALU.mult,
                                         op1=ALU.subtract).then_inc(t2_lo, 1)

            def gate_up_lo(fc, slot, n):
                dve.wait_ge(wgu_hi, n)
                low(wgu_hl[slot][:, 1], wgu_raw[slot][:], wgu_hl[slot][:, 0]).then_inc(wgu_lo, 1)
                dve.wait_ge(bgu_hi, n)
                dve.scalar_tensor_tensor(out=bgu_st[slot][:], in0=bgu_st[slot][:].bitcast(F32),
                                         scalar=lo_rows16[:, 0:1], in1=bgu_raw[slot][:],
                                         op0=ALU.mult, op1=ALU.add).then_inc(bgu_ready, 1)

            t2_low(0)
            split_lo("agu")
            residual(2, 0, [])
            t2_low(1)
            gate_up_lo(0, 0, 1)
            gate_up_lo(1, 1, 2)
            residual(2, 1, [])

            def t3_uv_low(h):
                cols = slice(h * HT, (h + 1) * HT)
                dve.wait_ge(t3_uv_hi, h + 1)
                low(t3_uv[2 * RG:4 * RG, cols], bank[h][0:2 * RG], t3_uv[0:2 * RG, cols]).then_inc(t3_uv_lo, 1)

            def t3_low(h):
                if h == 0:
                    dve.wait_ge(sel_in, 16)
                for i, (g, par) in enumerate(T3_BLOCKS):
                    dst, src = t3_block(h, g, par)
                    dve.wait_ge(t3_hi, 4 * h + i + 1)
                    dve.scalar_tensor_tensor(out=dst, in0=dst.bitcast(F32),
                                             scalar=sel_raw[64 * par:64 * par + 64, 2 * P:2 * P + 1],
                                             in1=src, op0=ALU.mult, op1=ALU.add).then_inc(t3_lo, 1)

            def mul_and_low(fc, h):
                n = 2 * fc + h
                cols = slice(h * HT, (h + 1) * HT)
                dve.wait_ge(silu_done, n + 1)
                dve.wait_ge(up_done, n + 1)
                dve.tensor_tensor(act_f[h][:], bank[5 + 2 * h][:], act_f[h][:], ALU.mult).then_inc(act_mul, 1)
                dve.wait_ge(act_hi, n + 1)
                low(act_hl[:, fc, 1, cols], act_f[h][:], act_hl[:, fc, 0, cols]).then_inc(act_lo, 1)

            def down_split_lo(name):
                _, _, raw, hl = down_splits[name]
                dve.wait_ge(down_hi, down_nth[name])
                low(hl[:, 1], raw[:], hl[:, 0]).then_inc(down_lo, 1)

            def td_low(h):
                dve.wait_ge(td_hi, 3 * h + 3)
                for par in range(2):
                    src, hi, lo = td_block(h, par)
                    if par == 1:
                        hi = td_odd[h][0:2 * R]
                    dve.scalar_tensor_tensor(out=lo, in0=src, scalar=SCALING, in1=hi.bitcast(F32), op0=ALU.mult,
                                             op1=ALU.subtract).then_inc(td_lo, 1)

            def x3_add(h, o):
                dst = x_f[:, o, h * HT:(h + 1) * HT]
                dve.wait_ge(down_done, C * h + o + 1)
                dve.tensor_tensor(dst, bank[4 + o][:], dst, ALU.add).then_inc(x3_sum, 1)

            t3_uv_low(0)
            t3_low(0)
            t3_uv_low(1)
            mul_and_low(0, 0)
            t3_low(1)
            mul_and_low(0, 1)
            with dve.Fori(0, 4) as i:
                for u in range(2):
                    fc = 2 * i + 1 + u
                    gate_up_lo(fc + 1, u, fc + 2)
                    for h in range(H):
                        mul_and_low(fc, h)
            dve.wait_ge(ad_hi, 1)
            low(ad_hl[:, :, :, 1], ad_raw[:], ad_hl[:, :, :, 0]).then_inc(ad_lo, 1)
            gate_up_lo(FC - 1, 0, FC)
            down_split_lo("wd_0")
            for fc in (FC - 2, FC - 1):
                for h in range(H):
                    mul_and_low(fc, h)
            down_split_lo("wd_1")
            down_split_lo("bd")
            td_low(0)
            down_split_lo("wd_2")
            down_split_lo("wd_3")
            for o in range(C):
                x3_add(0, o)
            td_low(1)
            for o in range(C):
                x3_add(1, o)

        @block.tensor
        def _(pe):
            def transposes(dst, srcs):
                for k, src in enumerate(srcs):
                    ins = pe.transpose(dst[:, k * P:(k + 1) * P], src, ident[:])
                return ins

            def transpose_y0(b):
                pe.wait_ge(y0_copied, b + 1)
                if b >= 2:
                    pe.wait_ge(x1_sum, b - 1)
                transposes(bank[2 + b % 2], [y0[b % 2][:, c * P:(c + 1) * P] for c in range(C)]).then_inc(l0_tr, 1)

            def thin1(h, j):
                b = HB * h + j
                cols = slice(b * S, (b + 1) * S)
                pe.wait_ge(x1_lo, b + 1)
                if h == 1:
                    pe.wait_ge(x1_sum, B)
                    pe.wait_ge(hg_lo, 1)
                for c in range(C):
                    for k in range(2):
                        ins = pe.matmul(thin1_bank(h, j)[:, 0:2 * TM1], xb[:, k, c, cols],
                                        aw1_hl[:, c].rearrange("p k n -> p (k n)"),
                                        start=(c == 0 and k == 0), stop=(c == C - 1 and k == 1))
                ins.then_inc(l1_tm, 1)

            pe.wait_ge(ident_ready, 1)
            for _ in range(WARM_UP):
                pe.matmul(bank[7][:, 0:P], ident[:], ident[:], start=True, stop=True)
            for b in range(B):
                cols = slice(b * S, (b + 1) * S)
                raw = w0_raw[b % W0_RING]
                pe.wait_ge(x_in[b], 16)
                if b >= 2:
                    pe.wait_ge(y0_copied, b - 1)
                if b == 0:
                    for c in range(C):
                        pe.wait_ge(w0c_in[c], 16)
                        ins = pe.matmul(bank[0][:], x_f[:, c, cols], raw[:, c], start=(c == 0), stop=(c == C - 1))
                else:
                    pe.wait_ge(w0_in[b % W0_RING][0], w0_landed(b))
                    pe.matmul(bank[b % 2][:], x_f[:, 0, cols], raw[:, 0], start=True,
                              stop=False).then_inc(w0_raw_used, 1)
                    pe.wait_ge(x0_lo, b)
                    hl = w0_hl[b % W0_RING]
                    for k in range(KC):
                        if k == 1:
                            transpose_y0(b - 1)
                        pe.wait_ge(w0_lo, KC * (b - 1) + k + 1)
                        pe.matmul(bank[b % 2][:], xa[:, 0, 1 + k, cols], hl[:, 0, k], start=False, stop=False)
                        pe.matmul(bank[b % 2][:], xa[:, 0, 1 + k, cols], hl[:, 1, k], start=False, stop=False)
                        ins = pe.matmul(bank[b % 2][:], xa[:, 1, 1 + k, cols], hl[:, 0, k], start=False,
                                        stop=(k == KC - 1))
                ins.then_inc(l0_tm, 1)
                if b == 3:
                    pe.wait_ge(w12_lo, nth["aw1"])
                if 3 <= b < 7:
                    thin1(0, b - 3)


            def split_product(dst, w_hi, w_lo, x, h, start, stop):
                cols = slice(h * HT, (h + 1) * HT)
                pe.matmul(dst, w_hi, x[0][:, cols], start=start, stop=False)
                pe.matmul(dst, w_hi, x[1][:, cols], start=False, stop=False)
                return pe.matmul(dst, w_lo, x[0][:, cols], start=False, stop=stop)

            def base(l, h, o):
                n = number(l, h, o)
                x, hl = (xb, w1_hl) if l == 1 else (xa, w2_hl)
                if n < 4:
                    pe.wait_ge(ranks_summed, n + 1)
                else:
                    pe.wait_ge(x_sum, n - 3)
                pe.wait_ge(w12_lo, nth[f"w{l}_{o}"])
                for c in range(C):
                    split_product(bank[4 + n % 4][:], hl[:, 0, o, c], hl[:, 1, o, c], (x[:, 0, c], x[:, 1, c]), h,
                                  c == 0, False)

            def lora1(h, o):
                n = number(1, h, o)
                cols = slice(o * P, (o + 1) * P)
                split_product(bank[4 + n % 4][:], b1_hl[:, 0, cols], b1_hl[:, 1, cols],
                              (hg_hl[:, 0], hg_hl[:, 1]), h, False, True).then_inc(main_done, 1)

            for h in range(H):
                if h == 1:
                    for j in range(HB):
                        thin1(1, j)
                for o in range(3):
                    base(1, h, o)
                    if h == 0 and o == 0:
                        transpose_y0(B - 1)
                pe.wait_ge(h_gated_ready, h + 1)
                transposes(bank[0], [h_gated[h][:, j] for j in range(HB)]).then_inc(l1_tr, 1)
                pe.wait_ge(w12_lo, nth["b1"])
                base(1, h, 3)
                pe.wait_ge(hg_lo, h + 1)
                for o in range(C):
                    lora1(h, o)

            def thin(h, a_hl, x):
                for j in range(HB):
                    b = HB * h + j
                    for c in range(C):
                        for k in range(2):
                            ins = pe.matmul(bank[h][0:64, j * S:(j + 1) * S],
                                            a_hl[:, b, c].rearrange("p k r -> p (k r)"),
                                            x[:, k, c, b * S:(b + 1) * S],
                                            start=(c == 0 and k == 0), stop=(c == C - 1 and k == 1))
                return ins

            def delta2(h, o):
                for k in range(2):
                    ins = pe.matmul(bank[4 + number(2, h, o) % 4][:], b2_hl[:, k, o * P:(o + 1) * P],
                                    t2_st[:, h * HT:(h + 1) * HT], start=False, stop=(k == 1))
                ins.then_inc(main_done, 1)

            pe.wait_ge(w12_lo, nth["a2"])
            for h in range(H):
                pe.wait_ge(x_lo, number(1, h, C - 1) + 1)
                thin(h, a2_hl, xa).then_inc(l2_tm, 1)
                base(2, h, 0)
                base(2, h, 1)
                pe.wait_ge(w12_lo, nth["b2"])
                pe.wait_ge(t2_lo, h + 1)
                delta2(h, 0)
                delta2(h, 1)
                for o in (2, 3):
                    base(2, h, o)
                    delta2(h, o)

            def thin3(h):
                pe.wait_ge(x_lo, number(2, h, C - 1) + 1)
                thin(h, agu_hl, xb).then_inc(l3_tm, 1)

            def sum_ranks(h):
                pe.wait_ge(sel_copied, 1)
                pe.wait_ge(t3_uv_lo, h + 1)
                if h == 1:
                    pe.wait_ge(t3_lo, 4)
                for g in range(2):
                    ins = pe.matmul(bank[2 + g][:], sel_r[:, g], t3_uv[:, h * HT:(h + 1) * HT], start=True, stop=True)
                ins.then_inc(t3_done, 1)

            def gate_up_main(g, h, slot):
                for c in range(C):
                    hl = wgu_hl[slot]
                    split_product(bank[4 + 2 * h + g][:], hl[:, 0, c, g], hl[:, 1, c, g],
                                  (xb[:, 0, c], xb[:, 1, c]), h, c == 0, False)

            def gate_up_lora(g, h, slot):
                for q in range(2):
                    pair = 2 * h + q
                    ins = pe.matmul(bank[4 + 2 * h + g][:, q * 2 * S:(q + 1) * 2 * S], bgu_st[slot][:, pair, g],
                                    t3_st[:, g, pair * 2 * S:(pair + 1) * 2 * S], start=False, stop=(q == 1))
                ins.then_inc(up_done if g else gate_done, 1)

            pe.wait_ge(w12_lo, nth["agu"])
            thin3(0)
            pe.wait_ge(wgu_lo, 1)
            pe.wait_ge(x_sum, number(2, 0, 0) + 1 + 5)
            gate_up_main(0, 0, 0)
            sum_ranks(0)
            gate_up_main(1, 0, 0)
            thin3(1)
            pe.wait_ge(bgu_ready, 1)
            pe.wait_ge(t3_lo, 4)
            for g in range(2):
                gate_up_lora(g, 0, 0)
            gate_up_main(0, 1, 0)
            sum_ranks(1)
            gate_up_main(1, 1, 0)
            pe.wait_ge(t3_lo, 8)
            for g in range(2):
                gate_up_lora(g, 1, 0)
            with pe.Fori(0, (FC - 1) // 2) as i:
                for u in range(2):
                    fc = 2 * i + 1 + u
                    slot = 1 - u
                    pe.wait_ge(wgu_lo, fc + 1)
                    pe.wait_ge(bgu_ready, fc + 1)
                    for h in range(H):
                        pe.wait_ge(silu_done, 2 * fc - 1 + h)
                        gate_up_main(0, h, slot)
                        gate_up_lora(0, h, slot)
                        pe.wait_ge(act_mul, 2 * fc - 1 + h)
                        gate_up_main(1, h, slot)
                        gate_up_lora(1, h, slot)

            def down_ranks(h):
                pe.wait_ge(act_lo, 2 * FC - 1 + h)
                for j in range(HB):
                    b = HB * h + j
                    for f in range(FC):
                        for k in range(2):
                            ins = pe.matmul(bank[h][0:2 * R, j * S:(j + 1) * S],
                                            ad_hl[:, b, f].rearrange("p k r -> p (k r)"),
                                            act_hl[:, f, k, b * S:(b + 1) * S],
                                            start=(f == 0 and k == 0), stop=(f == FC - 1 and k == 1))
                ins.then_inc(td_done, 1)

            def down_main(h, o):
                pe.wait_ge(down_lo, down_nth[f"wd_{o}"])
                if h == 0:
                    pe.wait_ge(act_mul, 2 * FC - 1 + o // 2)
                else:
                    pe.wait_ge(x3_sum, o + 1)
                for f in range(FC):
                    split_product(bank[4 + o][:], wd_hl[o][:, 0, f], wd_hl[o][:, 1, f],
                                  (act_hl[:, f, 0], act_hl[:, f, 1]), h, f == 0, False)

            def down_lora(h, o):
                for q in range(2):
                    pair = 2 * h + q
                    for k in range(2):
                        ins = pe.matmul(bank[4 + o][:, q * 2 * S:(q + 1) * 2 * S],
                                        bd_hl[:, k, pair, o * P:(o + 1) * P],
                                        td_st[:, pair * 2 * S:(pair + 1) * 2 * S], start=False,
                                        stop=(q == 1 and k == 1))
                ins.then_inc(down_done, 1)

            pe.wait_ge(ad_lo, 1)
            for h in range(H):
                down_ranks(h)
                for o in range(C):
                    down_main(h, o)
                    if h == 0 and o == 0:
                        pe.wait_ge(down_lo, down_nth["bd"])
                    if o == 0:
                        pe.wait_ge(td_lo, 2 * h + 2)
                    down_lora(h, o)


def kernel(**inputs):
    import numpy as np
    import concourse.bacc as bacc
    from concourse import mybir as mb
    from concourse.bass_utils import run_bass_kernel_spmd as run

    a = {k: np.asarray(v) for k, v in inputs.items()}

    def chunked(w):
        *lead, k, n = w.shape
        return np.moveaxis(w.reshape(*lead, k // P, P, n), -3, -2)

    def padded(w, axis):
        shape = list(w.shape)
        shape[axis] = FC * P
        z = np.zeros(shape, w.dtype)
        z[tuple(slice(0, n) for n in w.shape)] = w
        return z

    def stacked(w, copies):
        *lead, r, n = w.shape
        return np.broadcast_to(w[..., None, :, :], (*lead, copies, r, n)).reshape(*lead, copies * r, n)

    def rank_sums():
        row, col = np.arange(P), np.arange(2 * P)
        same = ((row[:, None] // R % 2) == (col // P)) & ((row[:, None] % R) == (col % R))
        part = -(row // R % 2)[:, None]
        return np.concatenate([same * SCALING, part], axis=1).astype(np.float32)

    t = lambda w: np.swapaxes(w, -1, -2)
    w_sq = lambda w: chunked(t(w)).reshape(P, C, C, P).transpose(0, 2, 1, 3)
    gu = lambda g, u: np.stack([g, u], axis=-2)
    bg, bu = (padded(t(a[f"L3_cond_B_{n}"][0]), 2).reshape(16, R, FC, P) for n in ("gate", "up"))
    wg, wu = (chunked(padded(t(a[f"L3_cond_W_{n}"]), 1)).reshape(P, C, FC, P) for n in ("gate", "up"))
    arrays = {
        "xT": chunked(t(a["x"])),
        "ids0": a["itok_B_0_15"][None], "ids1": a["itok_B_0_7"], "ids2": a["itok_B_0_4"][None],
        "ids3": a["itok_B_2_6"][None],
        "w0": chunked(t(a["L0_cond_weight"])).reshape(16, P, C * D),
        "w1": w_sq(a["L1_cond_W"]),
        "aw1": chunked(np.concatenate([t(a["L1_cond_A"].reshape(ER, D)), t(a["L1_cond_Wr"])], axis=1)),
        "b1": np.swapaxes(a["L1_cond_B"], 1, 2).reshape(ER, D),
        "w2": w_sq(a["L2_cond_weight"]),
        "a2": chunked(a["L2_cond_lora_A"]),
        "b2": stacked(t(a["L2_cond_lora_B"]), 4),
        "bias2": a["L2_cond_bias"].reshape(C, P).T,
        "wgu": gu(wg, wu).transpose(2, 0, 1, 3, 4),
        "agu": chunked(np.concatenate([t(a["L3_cond_A_gate"][0]), t(a["L3_cond_A_up"][0])], axis=2)),
        "sel": rank_sums(),
        "bgu": stacked(gu(bg, bu).transpose(0, 2, 1, 3, 4).reshape(16, FC, R, 2 * P), 4),
        "wd": chunked(padded(t(a["L3_cond_W_down"]), 0)).reshape(P, FC, C, P).transpose(2, 0, 1, 3),
        "ad": chunked(padded(t(a["L3_cond_A_down"][0]), 1)),
        "bd": stacked(t(a["L3_cond_B_down"][0]), 4),
    }
    nc = bacc.Bacc("TRN2", target_bir_lowering=False, num_devices=1, dynamic_dma_scratch_size=1024)
    feed, args = {}, []
    for name, v in arrays.items():
        v = np.ascontiguousarray(v)
        feed[f"in_{name}"] = v
        args.append(nc.dram_tensor(f"in_{name}", v.shape, mb.dt.from_np(v.dtype), kind="ExternalInput").ap())
    out = nc.dram_tensor("out_0", (C, P, T), mb.dt.float32, kind="ExternalOutput").ap()
    bass_four_residual_layers(nc, *args, out)
    y = run(nc, [feed], core_ids=[0]).results[0]["out_0"]
    return np.ascontiguousarray(y.reshape(D, B, S).transpose(1, 2, 0))
```

```python
from contextlib import ExitStack

import concourse.bass as bass
from concourse import mybir

F32 = mybir.dt.float32
F32R = mybir.dt.float32r
I32 = mybir.dt.int32
U32 = mybir.dt.uint32
ALU = mybir.AluOpType
ACT = mybir.ActivationFunctionType
AX_X = mybir.AxisListType.X

P = 128
B, S, D = 8, 128, 512
C = D // P
T = B * S
H = 2
HB = B // H
HT = T // H
E, R = 8, 16
ER = E * R
TM1 = ER + E
R2 = 32
RG = 2 * R
FC = 11
LANG_BIAS = 5.0
SCALING1 = 2.0
SCALING = 0.5
BANK = 512
KC = C - 1
WARM_UP = 9
W0_RING = 3


def bass_four_residual_layers(nc, xT, ids0, ids1, ids2, ids3, w0, w1, aw1, b1, w2, a2, b2, bias2,
                              wgu, agu, sel, bgu, wd, ad, bd, out):
    ctx = ExitStack()
    with ctx:
        base = (nc.sbuf_base + 31) // 32 * 32

        def at(name, off, shape, dt=F32):
            return nc.alloc_sbuf_tensor_at(name, [P, *shape], dt, offset=base + off)

        KB = 1024
        o_xf, o_xb, o_act = 0, 16 * KB, 48 * KB
        o_xa = o_act
        o_w0 = o_act + 32 * KB
        o_w1 = o_act + 56 * KB
        o_w2 = o_act + 72 * KB
        o_wgu = 136 * KB
        o_raw = o_wgu + 16 * KB
        o_slot2 = o_raw + 16 * KB
        o_bst = o_slot2 + 8 * KB
        o_tp = o_bst + 8 * KB
        o_ad = o_tp + 8 * KB
        o_misc = o_ad + 11 * KB

        x_f = at("x_f", o_xf, [C, T])
        xa = at("xa", o_xa, [2, C, T], F32R)
        xb = at("xb", o_xb, [2, C, T], F32R)
        w0_raw = [at(f"w0_raw{i}", o_raw + i * 8 * KB, [C, D]) for i in range(W0_RING)]
        w0_hl = [at(f"w0_hl{i}", (o_w0, o_w0 + 12 * KB, o_w2)[i], [2, KC, D], F32R)
                 for i in range(W0_RING)]
        y0 = [at(f"y0_{i}", o_tp + i * 2 * KB, [D]) for i in range(2)]
        w1_hl = at("w1_hl", o_w1, [2, C, C, P], F32R)
        aw1_hl = at("aw1_hl", o_wgu, [C, 2, TM1], F32R)
        b1_hl = at("b1_hl", o_wgu + 5 * KB, [2, D], F32R)
        aw1_raw = at("aw1_raw", o_bst, [C, TM1])
        b1_raw = at("b1_raw", o_bst + 3 * KB, [D])
        h_sum = [at(f"h_sum{i}", o_wgu + (9 + i * 3) * KB, [HB, TM1]) for i in range(H)]
        h_gated = [at(f"h_gated{i}", o_w0 + 20 * KB + i * 2 * KB, [HB, ER]) for i in range(H)]
        hg_hl = at("hg_hl", o_w0 + 12 * KB, [2, T], F32R)
        w2_raw = at("w2_raw", o_raw, [C, C, P])
        w2_hl = at("w2_hl", o_w2, [2, C, C, P], F32R)
        a2_raw = at("a2_raw", o_tp + 4 * KB, [B, C, R2])
        a2_hl = at("a2_hl", o_ad, [B, C, 2, R2], F32R)
        b2_raw = at("b2_raw", o_bst + 5 * KB, [D])
        b2_st = at("b2_st", o_slot2, [D], F32R)
        uv = at("uv", o_w0 + 16 * KB, [T], F32R)
        t2_st = at("t2_st", o_w0 + 12 * KB, [T], F32R)
        agu_raw = at("agu_raw", o_w0 + 8 * KB, [B, C, RG])
        agu_hl = at("agu_hl", o_w0, [B, C, 2, RG], F32R)
        t3_st = at("t3_st", o_tp, [2, T], F32R)
        bgu_raw = [at(f"bgu_raw{i}", o_raw + i * 4 * KB, [B // 2, 2, P]) for i in range(2)]
        wgu_raw = [at(f"wgu_raw{i}", o_raw + (8 + i * 4) * KB, [C, 2, P]) for i in range(2)]
        bgu_st = [at(f"bgu_st{i}", o_bst + i * 4 * KB, [B // 2, 2, P], F32R) for i in range(2)]
        wgu_hl = [at(f"wgu_hl{i}", o_wgu + i * 8 * KB, [2, C, 2, P], F32R) for i in range(2)]
        act_hl = at("act_hl", o_act, [FC, 2, T], F32R)
        act_f = [at(f"act_f{i}", o_slot2 + i * 2 * KB, [HT]) for i in range(2)]
        ad_raw = at("ad_raw", o_act + 80 * KB, [B, FC, R])
        ad_hl = at("ad_hl", o_ad, [B, FC, 2, R], F32R)
        td_st = at("td_st", o_slot2 + 4 * KB, [T], F32R)
        td_uv = [at(f"td_uv{i}", o_slot2 + 2 * i * KB, [HT], F32R) for i in range(H)]
        bd_raw = at("bd_raw", o_raw, [B // 2, D])
        bd_st = at("bd_st", o_bst, [B // 2, D], F32R)
        m = [o_misc]

        def own(name, shape, dt=F32):
            n = 4
            for k in shape:
                n *= k
            t = at(name, m[0], shape, dt)
            m[0] += (n + 31) // 32 * 32
            return t

        ident = own("ident", [P])
        wd_own = own("wd_own", [FC, P])
        wd_raw = [wd_own, at("wd_raw1", o_raw + 8 * KB, [FC, P]), wd_own, at("wd_raw3", o_xb + 22 * KB, [FC, P])]
        w1_raw = at("w1_raw", m[0], [C, C, P])
        wd_hl = [own("wd_hl0", [2, FC, P], F32R), at("wd_hl1", o_xb, [2, FC, P], F32R),
                 at("wd_hl2", o_xb + 11 * KB, [2, FC, P], F32R), at("wd_hl3", o_wgu, [2, FC, P], F32R)]
        sel_raw = at("sel_raw", o_slot2 + 5 * KB, [4 * P + 1])
        sel_r = own("sel_r", [4, P], F32R)
        hi_lo = own("hi_lo", [1])
        bias_sb = own("bias_sb", [C])
        lo_rows16 = own("lo_rows16", [1])
        lang_i = own("lang_i", [B], I32)
        lang_f = own("lang_f", [B])
        iota_e = own("iota_e", [E])
        assert base + m[0] <= nc.sbuf_usable_end, (base + m[0], nc.sbuf_usable_end)
        m[0] = o_wgu + 15 * KB
        lang_bias = own("lang_bias", [B, E])
        logits = own("logits", [HB, E])
        top_v = own("top_v", [HB, 8])
        top_i = own("top_i", [HB, 8], U32)
        top_f = own("top_f", [HB, 2])
        gap = own("gap", [HB])
        gap_e = own("gap_e", [HB])
        gate_w = own("gate_w", [4, HB])
        eq = at("eq", o_wgu + 11 * KB + KB // 2, [2, HB, E])
        assert m[0] <= o_raw

        bank = [ctx.enter_context(nc.psum_tensor(f"bank{i}", [P, BANK], F32)) for i in range(8)]

        def sem(name):
            return ctx.enter_context(nc.semaphore(name))

        x_in = [sem(f"x_in{b}") for b in range(B)]
        w0c_in = [sem(f"w0c_in{c}") for c in range(C)]
        w0_in = [[sem(f"w0_in{i}_{k}") for k in range(KC)] for i in range(W0_RING)]
        aw1_in, b1_in, lang_in = sem("aw1_in"), sem("b1_in"), sem("lang_in")
        w1_in = [sem(f"w1_in{o}") for o in range(C)]
        w2_in, a2_in, b2_in, bias_in = sem("w2_in"), sem("a2_in"), sem("b2_in"), sem("bias_in")
        agu_in, sel_in = sem("agu_in"), sem("sel_in")
        wgu_in = [sem(f"wgu_in{i}") for i in range(2)]
        bgu_in = [sem(f"bgu_in{i}") for i in range(2)]
        ad_in, bd_in = sem("ad_in"), sem("bd_in")
        wd_in = [sem(f"wd_in{o}") for o in range(C)]
        out_sent = sem("out_sent")
        const_step, ident_ready, masks_ready, iota_ready = (sem(n) for n in (
            "const_step", "ident_ready", "masks_ready", "iota_ready"))
        t3_zeroed, td_zeroed = sem("t3_zeroed"), sem("td_zeroed")
        x0_hi, x0_lo = sem("x0_hi"), sem("x0_lo")
        w0_raw_used, l0_tm, l0_tr = sem("w0_raw_used"), sem("l0_tm"), sem("l0_tr")
        l1_tm, l1_tr = sem("l1_tm"), sem("l1_tr")
        l2_tm, l3_tm, t2_done, t3_done = sem("l2_tm"), sem("l3_tm"), sem("t2_done"), sem("t3_done")
        main_done = sem("main_done")
        gate_done, up_done = sem("gate_done"), sem("up_done")
        td_tm, td_done, down_done = sem("td_tm"), sem("td_done"), sem("down_done")
        w0_hi, y0_copied, x1_hi = sem("w0_hi"), sem("y0_copied"), sem("x1_hi")
        w12_hi, gap_exp, hg_hi = sem("w12_hi"), sem("gap_exp"), sem("hg_hi")
        x_hi, t2_hi, t3_uv_hi, t3_hi = sem("x_hi"), sem("t2_hi"), sem("t3_uv_hi"), sem("t3_hi")
        sel_copied, t2_uv_hi, td_uv_hi = sem("sel_copied"), sem("t2_uv_hi"), sem("td_uv_hi")
        wgu_hi, bgu_hi, silu_done, act_hi = sem("wgu_hi"), sem("bgu_hi"), sem("silu_done"), sem("act_hi")
        ad_hi, down_hi, td_hi = sem("ad_hi"), sem("down_hi"), sem("td_hi")
        w0_lo, x1_sum, x1_lo = sem("w0_lo"), sem("x1_sum"), sem("x1_lo")
        ranks_summed = sem("ranks_summed")
        w12_lo, router_step, gap_ready, h_gated_ready = (sem(n) for n in (
            "w12_lo", "router_step", "gap_ready", "h_gated_ready"))
        hg_lo, x_sum, x_lo = sem("hg_lo"), sem("x_sum"), sem("x_lo")
        t2_lo, t3_uv_lo, t3_lo = sem("t2_lo"), sem("t3_uv_lo"), sem("t3_lo")
        t2_uv_lo, td_uv_lo, hi_lo_copied = sem("t2_uv_lo"), sem("td_uv_lo"), sem("hi_lo_copied")
        wgu_lo, bgu_ready, act_mul, act_lo = sem("wgu_lo"), sem("bgu_ready"), sem("act_mul"), sem("act_lo")
        ad_lo, down_lo, td_lo, x3_sum = sem("ad_lo"), sem("down_lo"), sem("td_lo"), sem("x3_sum")

        def w0_landed(b):
            return 16 * (b // W0_RING + (b % W0_RING > 0))

        def number(l, h, o):
            return 8 * (l - 1) + C * h + o

        def thin1_bank(h, j):
            return bank[4 + j if h == 0 else j]

        splits = ["aw1"] + [f"w1_{o}" for o in range(C)] + ["b1", "a2"] + [f"w2_{o}" for o in range(C)] + ["b2", "agu"]
        nth = {name: i + 1 for i, name in enumerate(splits)}

        def split_views(name):
            if name == "aw1":
                return aw1_raw[:], aw1_hl[:, :, 0], aw1_hl[:, :, 1]
            if name == "b1":
                return b1_raw[:], b1_hl[:, 0], b1_hl[:, 1]
            if name == "a2":
                return a2_raw[:], a2_hl[:, :, :, 0], a2_hl[:, :, :, 1]
            if name == "agu":
                return agu_raw[:], agu_hl[:, :, :, 0], agu_hl[:, :, :, 1]
            if name == "b2":
                return b2_raw[:], b2_st[:], None
            raw, hl = (w1_raw, w1_hl) if name[1] == "1" else (w2_raw, w2_hl)
            o = int(name[3:])
            return raw[:, o], hl[:, 0, o], hl[:, 1, o]

        split_source = {"aw1": (aw1_in, 16), "b1": (b1_in, 16), "a2": (a2_in, 16 * B), "agu": (agu_in, 16 * B),
                        "b2": (b2_in, 16)}
        for o in range(C):
            split_source[f"w1_{o}"] = (w1_in[o], 16)
            split_source[f"w2_{o}"] = (w2_in, 16)

        T3_BLOCKS = [(g, par) for g in range(2) for par in range(2)]

        def t3_block(h, g, par):
            rows = slice(64 * par, 64 * par + 64)
            dst = t3_st[rows, g, h * HT:(h + 1) * HT].rearrange("p (q b s) -> p q b s", b=2, s=S)
            src = bank[2 + g][rows].rearrange("p (q b s) -> p q b s", b=2, s=S)
            return dst[:, :, par], src[:, :, par]

        down_splits = {
            "wd_0": (wd_in[0], 16, wd_raw[0], wd_hl[0]), "wd_1": (wd_in[1], 16, wd_raw[1], wd_hl[1]),
            "bd": (bd_in, 16 * B, bd_raw, bd_st),
            "wd_2": (wd_in[2], 16, wd_raw[2], wd_hl[2]), "wd_3": (wd_in[3], 16, wd_raw[3], wd_hl[3])}
        down_nth = {name: i + 1 for i, name in enumerate(down_splits)}

        def td_block(h, par):
            rows = slice(64 * par, 64 * par + 64)
            dst = td_st[rows, h * HT:(h + 1) * HT].rearrange("p (q b s) -> p q b s", b=2, s=S)
            src = bank[2 + h][rows].rearrange("p (q b s) -> p q b s", b=2, s=S)
            return dst[:, :, par], src[:, :, par]

        DOWN_PIECES = [(o, slice(h * HT, (h + 1) * HT)) for h in range(H) for o in range(C)][:-1]
        DOWN_PIECES += [(C - 1, slice(first, first + 2 * S)) for first in (T - 4 * S, T - 2 * S)]

        def down_bank(o, cols):
            last = o == C - 1 and cols.start == T - 2 * S
            return bank[0 if last else 4 + o][:, cols.start % HT:(cols.stop - 1) % HT + 1]

        block = ctx.enter_context(nc.Block())

        @block.sync
        def _(sp):
            def id_of(src, b, last):
                return sp.value_load(src[0:1, b:b + 1], min_val=0, max_val=last)

            adapter = id_of(ids0, 0, w0.shape[0] - 1)
            for c in range(C):
                sp.dma_start(w0_raw[0][:, c], w0[adapter][:, c * D:(c + 1) * D]).then_inc(w0c_in[c], 16)
            for b in range(1, B):
                adapter = id_of(ids0, b, w0.shape[0] - 1)
                if b >= 2:
                    sp.dma_start(x_f[:, :, b * S:(b + 1) * S], xT[b]).then_inc(x_in[b], 16)
                if b == W0_RING:
                    sp.wait_ge(l0_tm, 1)
                if b > W0_RING:
                    sp.wait_ge(w0_raw_used, b - W0_RING)
                    sp.wait_ge(w0_lo, KC * (b - W0_RING))
                for k, (first, end) in enumerate(((0, 2), (2, 3), (3, 4))):
                    sp.dma_start(w0_raw[b % W0_RING][:, first:end],
                                 w0[adapter][:, first * D:end * D]).then_inc(w0_in[b % W0_RING][k], 16)
                if b == 2:
                    sp.dma_start(aw1_raw[:], aw1).then_inc(aw1_in, 16)
                    sp.dma_start(lang_i[:], ids1.partition_broadcast(P)).then_inc(lang_in, 16)
            for o in range(C):
                sp.dma_start(w1_raw[:, o], w1[:, o]).then_inc(w1_in[o], 16)
            sp.dma_start(b1_raw[:], b1).then_inc(b1_in, 16)
            sp.wait_ge(w0_raw_used, 6)
            sp.wait_ge(w0_lo, KC * 6)
            sp.dma_start(w2_raw[:], w2).then_inc(w2_in, 16)
            for b in range(B):
                sp.dma_start(a2_raw[:, b], a2[id_of(ids2, b, a2.shape[0] - 1)]).then_inc(a2_in, 16)
            sp.dma_start(b2_raw[:], b2).then_inc(b2_in, 16)
            sp.dma_start(bias_sb[:], bias2).then_inc(bias_in, 16)
            sp.dma_start(sel_raw[:], sel).then_inc(sel_in, 16)
            adapter3 = [id_of(ids3, b, agu.shape[0] - 1) for b in range(B)]
            sp.wait_ge(l0_tm, 8)
            for b in range(B):
                sp.dma_start(agu_raw[:, b], agu[adapter3[b]]).then_inc(agu_in, 16)

            def load_gate_up(fc, slot):
                sp.dma_start(wgu_raw[slot][:], wgu[fc]).then_inc(wgu_in[slot], 16)
                for b in range(B):
                    rows = slice(64 * (b % 2), 64 * (b % 2) + 64)
                    sp.dma_start(bgu_raw[slot][rows, b // 2], bgu[adapter3[b], fc]).then_inc(bgu_in[slot], 16)

            sp.wait_ge(w12_lo, nth["w2_3"])
            load_gate_up(0, 0)
            load_gate_up(1, 1)
            with sp.Fori(0, 4) as i:
                for u in range(2):
                    fc = 2 * i + 2 + u
                    sp.wait_ge(wgu_lo, 2 * i + 1 + u)
                    sp.wait_ge(bgu_ready, 2 * i + 1 + u)
                    load_gate_up(fc, u)
            sp.wait_ge(wgu_lo, FC - 2)
            sp.wait_ge(bgu_ready, FC - 2)
            load_gate_up(FC - 1, 0)
            for b in range(B):
                sp.dma_start(ad_raw[:, b], ad[adapter3[b]]).then_inc(ad_in, 16)
            sp.dma_start(wd_raw[0][:], wd[0]).then_inc(wd_in[0], 16)
            sp.wait_ge(wgu_lo, FC)
            sp.wait_ge(bgu_ready, FC)
            sp.dma_start(wd_raw[1][:], wd[1]).then_inc(wd_in[1], 16)
            for b in range(B):
                rows = slice(64 * (b % 2), 64 * (b % 2) + 64)
                sp.dma_start(bd_raw[rows, b // 2], bd[adapter3[b]]).then_inc(bd_in, 16)
            sp.wait_ge(down_lo, down_nth["wd_0"])
            sp.dma_start(wd_raw[2][:], wd[2]).then_inc(wd_in[2], 16)
            sp.wait_ge(up_done, 2 * FC)
            sp.dma_start(wd_raw[3][:], wd[3]).then_inc(wd_in[3], 16)
            for i, (o, cols) in enumerate(DOWN_PIECES):
                sp.wait_ge(x3_sum, i + 1)
                sp.dma_start(out[o, :, cols], x_f[:, o, cols]).then_inc(out_sent, 16)
            sp.wait_ge(out_sent, 16 * len(DOWN_PIECES))

        @block.gpsimd
        def _(pool):
            pool.memset(ident[:], 0.0).then_inc(const_step, 1)
            pool.wait_ge(const_step, 1)
            pool.affine_select(out=ident[:], in_=ident[:], compare_op=ALU.not_equal, fill=1.0, base=0,
                               pattern=[[-1, P]], channel_multiplier=1).then_inc(ident_ready, 1)
            pool.iota(iota_e[:], [[1, E]], base=0, channel_multiplier=0,
                      allow_small_or_imprecise_dtypes=True).then_inc(iota_ready, 1)
            for b in range(1, B):
                cols = slice(b * S, (b + 1) * S)
                pool.wait_ge(x_in[b], 16)
                pool.tensor_copy(xa[:, 0, 1:C, cols], x_f[:, 1:C, cols]).then_inc(x0_hi, 1)
                pool.wait_ge(x0_hi, b)
                pool.tensor_tensor(xa[:, 1, 1:C, cols], x_f[:, 1:C, cols],
                                   xa[:, 0, 1:C, cols].bitcast(F32), ALU.subtract).then_inc(x0_lo, 1)
            pool.wait_ge(l0_tr, B)
            pool.wait_ge(w12_lo, nth["a2"])
            pool.memset(t3_st[:].bitcast(F32), 0.0).then_inc(t3_zeroed, 1)
            pool.wait_ge(sel_copied, 1)
            pool.wait_ge(hi_lo_copied, 1)
            pool.memset(td_st[:].bitcast(F32), 0.0).then_inc(td_zeroed, 1)

        @block.scalar
        def _(act):
            def high(dst, src):
                return act.activation(dst, src, ACT.Copy)

            def split_hi(name):
                s, n = split_source[name]
                act.wait_ge(s, n)
                raw, hi, _ = split_views(name)
                high(hi, raw).then_inc(w12_hi, 1)

            def copy_y0(b):
                act.wait_ge(l0_tm, b + 1)
                if b >= 2:
                    act.wait_ge(l0_tr, b - 1)
                act.activation(y0[b % 2][:], bank[b % 2][:], ACT.Copy).then_inc(y0_copied, 1)

            def x1_high(b):
                cols = slice(b * S, (b + 1) * S)
                act.wait_ge(x1_sum, b + 1)
                high(xb[:, 0, :, cols], x_f[:, :, cols]).then_inc(x1_hi, 1)

            for b in range(2):
                act.dma_start(x_f[:, :, b * S:(b + 1) * S], xT[b]).then_inc(x_in[b], 16)
            for b in range(1, B):
                if b > W0_RING:
                    act.wait_ge(l0_tm, b - W0_RING + 1)
                if b == 3:
                    split_hi("aw1")
                for k in range(KC):
                    if k == KC - 1:
                        copy_y0(b - 1)
                    act.wait_ge(w0_in[b % W0_RING][k], w0_landed(b))
                    high(w0_hl[b % W0_RING][:, 0, k], w0_raw[b % W0_RING][:, 1 + k]).then_inc(w0_hi, 1)
                if b == 7:
                    split_hi("w1_0")
                    split_hi("w1_1")
                if b >= 2:
                    x1_high(b - 2)
            split_hi("w1_2")
            copy_y0(7)
            x1_high(6)
            split_hi("w1_3")
            split_hi("b1")

            def router_exp(h):
                act.wait_ge(gap_ready, h + 1)
                act.activation(gap_e[:], gap[:], ACT.Exp).then_inc(gap_exp, 1)

            def hg_high(h):
                act.wait_ge(l1_tr, h + 1)
                high(hg_hl[:, 0, h * HT:(h + 1) * HT], bank[0][:]).then_inc(hg_hi, 1)

            def x_high(l, h, o):
                n = number(l, h, o)
                dst = (xa if l == 1 else xb)[:, 0, o, h * HT:(h + 1) * HT]
                act.wait_ge(x_sum, n + 1)
                high(dst, x_f[:, o, h * HT:(h + 1) * HT]).then_inc(x_hi, 1)

            router_exp(0)
            x1_high(7)
            hg_high(0)
            split_hi("a2")
            for o in range(C):
                x_high(1, 0, o)
                split_hi(f"w2_{o}")
            router_exp(1)
            hg_high(1)
            split_hi("b2")
            for o in range(C):
                x_high(1, 1, o)

            def t2_uv_high(h):
                act.wait_ge(l2_tm, h + 1)
                high(uv[0:2 * R2, h * HT:(h + 1) * HT], bank[h][0:2 * R2]).then_inc(t2_uv_hi, 1)

            def t2_high(h):
                act.wait_ge(t2_done, h + 1)
                high(t2_st[:, h * HT:(h + 1) * HT], bank[2 + h][:]).then_inc(t2_hi, 1)

            def gate_up_hi(fc, slot, uses, free):
                act.wait_ge(wgu_in[slot], 16 * uses)
                if free is not None:
                    act.wait_ge(up_done, free)
                high(wgu_hl[slot][:, 0], wgu_raw[slot][:]).then_inc(wgu_hi, 1)
                act.wait_ge(bgu_in[slot], 16 * B * uses)
                high(bgu_st[slot][:], bgu_raw[slot][:]).then_inc(bgu_hi, 1)

            t2_uv_high(0)
            act.wait_ge(sel_in, 16)
            high(sel_r[:], sel_raw[:, 0:4 * P].rearrange("p (g m) -> p g m", g=4)).then_inc(sel_copied, 1)
            split_hi("agu")
            t2_high(0)
            for o in range(C):
                x_high(2, 0, o)
            t2_uv_high(1)
            gate_up_hi(0, 0, 1, None)
            t2_high(1)
            gate_up_hi(1, 1, 1, None)
            for o in range(C):
                x_high(2, 1, o)

            def t3_uv_high(h):
                act.wait_ge(l3_tm, h + 1)
                high(uv[0:2 * RG, h * HT:(h + 1) * HT], bank[h][0:2 * RG]).then_inc(t3_uv_hi, 1)

            def t3_high(h):
                act.wait_ge(t3_done, h + 1)
                act.wait_ge(t3_zeroed, 1)
                for g, par in T3_BLOCKS:
                    dst, src = t3_block(h, g, par)
                    high(dst, src).then_inc(t3_hi, 1)

            def silu(fc, h):
                act.wait_ge(gate_done, 2 * fc + h + 1)
                act.activation(act_f[h][:], bank[4 + 2 * h][:], ACT.Silu).then_inc(silu_done, 1)

            def act_high(fc, h):
                act.wait_ge(act_mul, 2 * fc + h + 1)
                high(act_hl[:, fc, 0, h * HT:(h + 1) * HT], act_f[h][:]).then_inc(act_hi, 1)

            def down_split_hi(name):
                s, n, raw, hl = down_splits[name]
                act.wait_ge(s, n)
                high(hl[:] if name == "bd" else hl[:, 0], raw[:]).then_inc(down_hi, 1)

            def td_uv_high(h):
                act.wait_ge(td_tm, h + 1)
                high(td_uv[h][0:2 * R], bank[h][0:2 * R]).then_inc(td_uv_hi, 1)

            def td_high(h):
                act.wait_ge(td_done, h + 1)
                act.wait_ge(td_zeroed, 1)
                for par in range(2):
                    dst, src = td_block(h, par)
                    high(dst, src).then_inc(td_hi, 1)

            t3_uv_high(0)
            t3_high(0)
            t3_uv_high(1)
            silu(0, 0)
            t3_high(1)
            act_high(0, 0)
            silu(0, 1)
            act_high(0, 1)
            with act.Fori(0, 4) as i:
                for u in range(2):
                    fc = 2 * i + 1 + u
                    gate_up_hi(fc + 1, u, i + 2 if u == 0 else i + 2, 4 * i + 2 + 2 * u)
                    for h in range(H):
                        if h == 0:
                            act.wait_ge(act_lo, 2 * fc - 1)
                        else:
                            act.wait_ge(act_lo, 2 * fc)
                        silu(fc, h)
                        act_high(fc, h)
            act.wait_ge(ad_in, 16 * B)
            high(ad_hl[:, :, :, 0], ad_raw[:]).then_inc(ad_hi, 1)
            gate_up_hi(FC - 1, 0, 6, 2 * (FC - 2))
            down_split_hi("wd_0")
            for fc in (FC - 2, FC - 1):
                for h in range(H):
                    act.wait_ge(act_lo, 2 * fc - 1 + h)
                    silu(fc, h)
                    act_high(fc, h)
            act.wait_ge(up_done, 2 * FC)
            down_split_hi("wd_1")
            down_split_hi("bd")
            act.wait_ge(act_lo, 2 * FC)
            td_uv_high(0)
            down_split_hi("wd_2")
            td_high(0)
            down_split_hi("wd_3")
            td_uv_high(1)
            td_high(1)

        @block.vector
        def _(dve):
            def low(dst, src, hi):
                return dve.tensor_tensor(dst, src, hi.bitcast(F32), ALU.subtract)

            def split_lo(name):
                raw, hi, lo = split_views(name)
                dve.wait_ge(w12_hi, nth[name])
                if name == "b2":
                    low(hi[64:P], raw[64:P], hi[64:P]).then_inc(w12_lo, 1)
                else:
                    low(lo, raw, hi).then_inc(w12_lo, 1)

            def x1_add(b):
                cols = slice(b * S, (b + 1) * S)
                dve.wait_ge(l0_tr, b + 1)
                dve.tensor_tensor(x_f[:, :, cols], bank[2 + b % 2][:].rearrange("p (c t) -> p c t", c=C),
                                  x_f[:, :, cols], ALU.add).then_inc(x1_sum, 1)

            def x1_low(b):
                cols = slice(b * S, (b + 1) * S)
                dve.wait_ge(x1_hi, b + 1)
                low(xb[:, 1, :, cols], x_f[:, :, cols], xb[:, 0, :, cols]).then_inc(x1_lo, 1)

            def sum_ranks1(h, j):
                dve.wait_ge(l1_tm, HB * h + j + 1)
                dve.tensor_reduce(h_sum[h][:, j], thin1_bank(h, j)[:, 0:2 * TM1].rearrange(
                    "p (k n) -> p n k", k=2), AX_X, ALU.add).then_inc(ranks_summed, 1)

            steps = [0]

            def step(ins):
                steps[0] += 1
                ins.then_inc(router_step, 1)
                dve.wait_ge(router_step, steps[0])

            def bias_of_language():
                dve.wait_ge(lang_in, 16)
                dve.wait_ge(iota_ready, 1)
                step(dve.tensor_copy(lang_f[:], lang_i[:]))
                step(dve.tensor_tensor(lang_bias[:], iota_e[:].unsqueeze(1).to_broadcast([P, B, E]),
                                       lang_f[:].unsqueeze(2).to_broadcast([P, B, E]), ALU.is_equal))
                step(dve.tensor_scalar(lang_bias[:], lang_bias[:], LANG_BIAS, None, ALU.mult))

            for q in range(4):
                last = dve.memset(lo_rows16[32 * q:32 * q + 32], -1.0 * (q % 2))
            last.then_inc(masks_ready, 1)
            for b in range(1, B):
                if b == 3:
                    split_lo("aw1")
                for k in range(KC):
                    dve.wait_ge(w0_hi, KC * (b - 1) + k + 1)
                    low(w0_hl[b % W0_RING][:, 1, k], w0_raw[b % W0_RING][:, 1 + k],
                        w0_hl[b % W0_RING][:, 0, k]).then_inc(w0_lo, 1)
                if b == 7:
                    split_lo("w1_0")
                    split_lo("w1_1")
                x1_add(b - 1)
                if b >= 2:
                    x1_low(b - 2)
                if b == 4:
                    bias_of_language()
                if b >= 5:
                    sum_ranks1(0, b - 5)
            split_lo("w1_2")
            sum_ranks1(0, 3)

            def router(h):
                bcast = [P, HB, E]
                if h == 1:
                    for j in range(HB):
                        sum_ranks1(1, j)
                dve.wait_ge(ranks_summed, HB * h + HB)
                step(dve.tensor_tensor(logits[:], h_sum[h][:, :, ER:TM1], lang_bias[:, HB * h:HB * h + HB], ALU.add))
                for j in range(HB):
                    ins = dve.max(top_v[:, j], logits[:, j])
                step(ins)
                if h == 1:
                    dve.wait_ge(gap_exp, 1)
                dve.tensor_tensor(gap[:], top_v[:, :, 1], top_v[:, :, 0], ALU.subtract).then_inc(gap_ready, 1)
                for j in range(HB):
                    ins = dve.max_index(top_i[:, j], top_v[:, j], logits[:, j])
                step(ins)
                step(dve.tensor_copy(top_f[:], top_i[:, :, 0:2]))
                for k in range(2):
                    dve.tensor_tensor(eq[:, k], iota_e[:].unsqueeze(1).to_broadcast(bcast),
                                      top_f[:, :, k:k + 1].to_broadcast(bcast), ALU.is_equal)
                dve.wait_ge(gap_exp, h + 1)
                step(dve.tensor_scalar(gate_w[:, 0], gap_e[:], 1.0, None, ALU.add))
                step(dve.reciprocal(gate_w[:, 1], gate_w[:, 0]))
                step(dve.tensor_scalar(gate_w[:, 2], gate_w[:, 1], SCALING1, None, ALU.mult))
                step(dve.tensor_tensor(gate_w[:, 3], gate_w[:, 2], gap_e[:], ALU.mult))
                for k in range(2):
                    ins = dve.tensor_tensor(eq[:, k], eq[:, k],
                                            gate_w[:, 2 + k].unsqueeze(2).to_broadcast(bcast), ALU.mult)
                step(ins)
                step(dve.tensor_tensor(logits[:], eq[:, 0], eq[:, 1], ALU.add))
                dve.tensor_tensor(h_gated[h][:].rearrange("p j (e r) -> p j e r", e=E),
                                  h_sum[h][:, :, 0:ER].rearrange("p j (e r) -> p j e r", e=E),
                                  logits[:].unsqueeze(3).to_broadcast([P, HB, E, R]),
                                  ALU.mult).then_inc(h_gated_ready, 1)

            def hg_low(h):
                cols = slice(h * HT, (h + 1) * HT)
                dve.wait_ge(hg_hi, h + 1)
                low(hg_hl[:, 1, cols], bank[0][:], hg_hl[:, 0, cols]).then_inc(hg_lo, 1)

            def x_add(l, h, o):
                n = number(l, h, o)
                dst = x_f[:, o, h * HT:(h + 1) * HT]
                dve.wait_ge(main_done, n + 1)
                if l == 1:
                    ins = dve.tensor_tensor(dst, bank[4 + n % 4][:], dst, ALU.add)
                else:
                    ins = dve.scalar_tensor_tensor(out=dst, in0=bank[4 + n % 4][:], scalar=bias_sb[:, o:o + 1],
                                                   in1=dst, op0=ALU.add, op1=ALU.add)
                ins.then_inc(x_sum, 1)

            def x_low(l, h, o):
                cols = slice(h * HT, (h + 1) * HT)
                xs = xa if l == 1 else xb
                dve.wait_ge(x_hi, number(l, h, o) + 1)
                low(xs[:, 1, o, cols], x_f[:, o, cols], xs[:, 0, o, cols]).then_inc(x_lo, 1)

            router(0)
            split_lo("w1_3")
            x1_add(7)
            x1_low(6)
            x1_low(7)
            split_lo("b1")
            hg_low(0)
            split_lo("a2")

            def residual(l, h, between):
                for o in range(C + 1):
                    if o < C:
                        x_add(l, h, o)
                    if o > 0:
                        x_low(l, h, o - 1)
                        if between:
                            split_lo(between.pop(0))

            residual(1, 0, ["w2_0", "w2_1", "w2_2"])
            router(1)
            split_lo("w2_3")
            hg_low(1)
            split_lo("b2")
            residual(1, 1, [])
            dve.wait_ge(bias_in, 16)

            def t2_uv_low(h):
                cols = slice(h * HT, (h + 1) * HT)
                dve.wait_ge(t2_uv_hi, h + 1)
                low(uv[2 * R2:4 * R2, cols], bank[h][0:2 * R2], uv[0:2 * R2, cols]).then_inc(t2_uv_lo, 1)

            def t2_low(h):
                cols = slice(h * HT, (h + 1) * HT)
                dve.wait_ge(masks_ready, 1)
                dve.wait_ge(t2_hi, h + 1)
                dve.scalar_tensor_tensor(out=t2_st[:, cols], in0=t2_st[:, cols].bitcast(F32),
                                         scalar=lo_rows16[:, 0:1], in1=bank[2 + h][:], op0=ALU.mult,
                                         op1=ALU.add).then_inc(t2_lo, 1)

            def gate_up_lo(fc, slot, n):
                dve.wait_ge(wgu_hi, n)
                low(wgu_hl[slot][:, 1], wgu_raw[slot][:], wgu_hl[slot][:, 0]).then_inc(wgu_lo, 1)
                dve.wait_ge(bgu_hi, n)
                dve.scalar_tensor_tensor(out=bgu_st[slot][:], in0=bgu_st[slot][:].bitcast(F32),
                                         scalar=lo_rows16[:, 0:1], in1=bgu_raw[slot][:],
                                         op0=ALU.mult, op1=ALU.add).then_inc(bgu_ready, 1)

            t2_uv_low(0)
            dve.wait_ge(sel_in, 16)
            dve.tensor_copy(hi_lo[:], sel_raw[:, 4 * P:4 * P + 1]).then_inc(hi_lo_copied, 1)
            split_lo("agu")
            t2_low(0)
            residual(2, 0, [])
            t2_uv_low(1)
            gate_up_lo(0, 0, 1)
            t2_low(1)
            gate_up_lo(1, 1, 2)
            residual(2, 1, [])

            def t3_uv_low(h):
                cols = slice(h * HT, (h + 1) * HT)
                dve.wait_ge(t3_uv_hi, h + 1)
                low(uv[2 * RG:4 * RG, cols], bank[h][0:2 * RG], uv[0:2 * RG, cols]).then_inc(t3_uv_lo, 1)

            def t3_low(h):
                if h == 0:
                    dve.wait_ge(hi_lo_copied, 1)
                for i, (g, par) in enumerate(T3_BLOCKS):
                    dst, src = t3_block(h, g, par)
                    dve.wait_ge(t3_hi, 4 * h + i + 1)
                    dve.scalar_tensor_tensor(out=dst, in0=dst.bitcast(F32),
                                             scalar=hi_lo[64 * par:64 * par + 64, 0:1],
                                             in1=src, op0=ALU.mult, op1=ALU.add).then_inc(t3_lo, 1)

            def act_product(fc, h):
                n = 2 * fc + h
                dve.wait_ge(silu_done, n + 1)
                dve.wait_ge(up_done, n + 1)
                dve.tensor_tensor(act_f[h][:], bank[5 + 2 * h][:], act_f[h][:], ALU.mult).then_inc(act_mul, 1)

            def act_low(fc, h):
                cols = slice(h * HT, (h + 1) * HT)
                dve.wait_ge(act_hi, 2 * fc + h + 1)
                low(act_hl[:, fc, 1, cols], act_f[h][:], act_hl[:, fc, 0, cols]).then_inc(act_lo, 1)

            def down_split_lo(name):
                _, _, raw, hl = down_splits[name]
                dve.wait_ge(down_hi, down_nth[name])
                if name == "bd":
                    dve.scalar_tensor_tensor(out=hl[:], in0=hl[:].bitcast(F32), scalar=lo_rows16[:, 0:1],
                                             in1=raw[:], op0=ALU.mult, op1=ALU.add).then_inc(down_lo, 1)
                else:
                    low(hl[:, 1], raw[:], hl[:, 0]).then_inc(down_lo, 1)

            def td_uv_low(h):
                dve.wait_ge(td_uv_hi, h + 1)
                low(td_uv[h][2 * R:4 * R], bank[h][0:2 * R], td_uv[h][0:2 * R]).then_inc(td_uv_lo, 1)

            def td_low(h):
                dve.wait_ge(td_hi, 2 * h + 2)
                for par in range(2):
                    dst, src = td_block(h, par)
                    dve.scalar_tensor_tensor(out=dst, in0=dst.bitcast(F32), scalar=hi_lo[64 * par:64 * par + 64, 0:1],
                                             in1=src, op0=ALU.mult, op1=ALU.add).then_inc(td_lo, 1)

            def x3_add(i):
                o, cols = DOWN_PIECES[i]
                dst = x_f[:, o, cols]
                dve.wait_ge(down_done, i + 1)
                dve.tensor_tensor(dst, down_bank(o, cols), dst, ALU.add).then_inc(x3_sum, 1)

            t3_uv_low(0)
            t3_low(0)
            t3_uv_low(1)
            act_product(0, 0)
            t3_low(1)
            act_low(0, 0)
            act_product(0, 1)
            act_low(0, 1)
            with dve.Fori(0, 4) as i:
                for u in range(2):
                    fc = 2 * i + 1 + u
                    gate_up_lo(fc + 1, u, fc + 2)
                    for h in range(H):
                        act_product(fc, h)
                        act_low(fc, h)
            dve.wait_ge(ad_hi, 1)
            low(ad_hl[:, :, :, 1], ad_raw[:], ad_hl[:, :, :, 0]).then_inc(ad_lo, 1)
            gate_up_lo(FC - 1, 0, FC)
            down_split_lo("wd_0")
            for fc in (FC - 2, FC - 1):
                for h in range(H):
                    act_product(fc, h)
                    act_low(fc, h)
            down_split_lo("wd_1")
            down_split_lo("bd")
            td_uv_low(0)
            down_split_lo("wd_2")
            td_low(0)
            down_split_lo("wd_3")
            for i in range(C):
                x3_add(i)
            td_uv_low(1)
            td_low(1)
            for i in range(C, len(DOWN_PIECES)):
                x3_add(i)

        @block.tensor
        def _(pe):
            def transposes(dst, srcs):
                for k, src in enumerate(srcs):
                    ins = pe.transpose(dst[:, k * P:(k + 1) * P], src, ident[:])
                return ins

            def transpose_y0(b):
                pe.wait_ge(y0_copied, b + 1)
                if b >= 2:
                    pe.wait_ge(x1_sum, b - 1)
                transposes(bank[2 + b % 2], [y0[b % 2][:, c * P:(c + 1) * P] for c in range(C)]).then_inc(l0_tr, 1)

            def thin1(h, j):
                b = HB * h + j
                cols = slice(b * S, (b + 1) * S)
                pe.wait_ge(x1_lo, b + 1)
                if h == 1:
                    pe.wait_ge(x1_sum, B)
                    pe.wait_ge(hg_lo, 1)
                for c in range(C):
                    for k in range(2):
                        ins = pe.matmul(thin1_bank(h, j)[:, 0:2 * TM1], xb[:, k, c, cols],
                                        aw1_hl[:, c].rearrange("p k n -> p (k n)"),
                                        start=(c == 0 and k == 0), stop=(c == C - 1 and k == 1))
                ins.then_inc(l1_tm, 1)

            pe.wait_ge(ident_ready, 1)
            for _ in range(WARM_UP):
                pe.matmul(bank[7][:, 0:P], ident[:], ident[:], start=True, stop=True)
            for b in range(B):
                cols = slice(b * S, (b + 1) * S)
                raw = w0_raw[b % W0_RING]
                pe.wait_ge(x_in[b], 16)
                if b >= 2:
                    pe.wait_ge(y0_copied, b - 1)
                if b == 0:
                    for c in range(C):
                        pe.wait_ge(w0c_in[c], 16)
                        ins = pe.matmul(bank[0][:], x_f[:, c, cols], raw[:, c], start=(c == 0), stop=(c == C - 1))
                else:
                    pe.wait_ge(w0_in[b % W0_RING][0], w0_landed(b))
                    pe.matmul(bank[b % 2][:], x_f[:, 0, cols], raw[:, 0], start=True,
                              stop=False).then_inc(w0_raw_used, 1)
                    pe.wait_ge(x0_lo, b)
                    hl = w0_hl[b % W0_RING]
                    for k in range(KC):
                        if k == 1:
                            transpose_y0(b - 1)
                        pe.wait_ge(w0_lo, KC * (b - 1) + k + 1)
                        pe.matmul(bank[b % 2][:], xa[:, 0, 1 + k, cols], hl[:, 0, k], start=False, stop=False)
                        pe.matmul(bank[b % 2][:], xa[:, 0, 1 + k, cols], hl[:, 1, k], start=False, stop=False)
                        ins = pe.matmul(bank[b % 2][:], xa[:, 1, 1 + k, cols], hl[:, 0, k], start=False,
                                        stop=(k == KC - 1))
                ins.then_inc(l0_tm, 1)
                if b == 3:
                    pe.wait_ge(w12_lo, nth["aw1"])
                if 3 <= b < 7:
                    thin1(0, b - 3)


            def split_product(dst, w_hi, w_lo, x, h, start, stop, cols=None):
                if cols is None:
                    cols = slice(h * HT, (h + 1) * HT)
                pe.matmul(dst, w_hi, x[0][:, cols], start=start, stop=False)
                pe.matmul(dst, w_hi, x[1][:, cols], start=False, stop=False)
                return pe.matmul(dst, w_lo, x[0][:, cols], start=False, stop=stop)

            def base(l, h, o):
                n = number(l, h, o)
                x, hl = (xb, w1_hl) if l == 1 else (xa, w2_hl)
                if n < 4:
                    pe.wait_ge(ranks_summed, n + 1)
                else:
                    pe.wait_ge(x_sum, n - 3)
                pe.wait_ge(w12_lo, nth[f"w{l}_{o}"])
                for c in range(C):
                    split_product(bank[4 + n % 4][:], hl[:, 0, o, c], hl[:, 1, o, c], (x[:, 0, c], x[:, 1, c]), h,
                                  c == 0, False)

            def lora1(h, o):
                n = number(1, h, o)
                cols = slice(o * P, (o + 1) * P)
                split_product(bank[4 + n % 4][:], b1_hl[:, 0, cols], b1_hl[:, 1, cols],
                              (hg_hl[:, 0], hg_hl[:, 1]), h, False, True).then_inc(main_done, 1)

            for h in range(H):
                if h == 1:
                    for j in range(HB):
                        thin1(1, j)
                for o in range(3):
                    base(1, h, o)
                    if h == 0 and o == 0:
                        transpose_y0(B - 1)
                pe.wait_ge(h_gated_ready, h + 1)
                transposes(bank[0], [h_gated[h][:, j] for j in range(HB)]).then_inc(l1_tr, 1)
                base(1, h, 3)
                pe.wait_ge(w12_lo, nth["b1"])
                pe.wait_ge(hg_lo, h + 1)
                for o in range(C):
                    lora1(h, o)

            def thin(h, a_hl, x):
                for j in range(HB):
                    b = HB * h + j
                    for c in range(C):
                        for k in range(2):
                            ins = pe.matmul(bank[h][0:64, j * S:(j + 1) * S],
                                            a_hl[:, b, c].rearrange("p k r -> p (k r)"),
                                            x[:, k, c, b * S:(b + 1) * S],
                                            start=(c == 0 and k == 0), stop=(c == C - 1 and k == 1))
                return ins

            def delta2(h, o):
                pe.matmul(bank[4 + number(2, h, o) % 4][:], b2_st[:, o * P:(o + 1) * P],
                          t2_st[:, h * HT:(h + 1) * HT], start=False, stop=True).then_inc(main_done, 1)

            pe.wait_ge(w12_lo, nth["a2"])
            for h in range(H):
                pe.wait_ge(x_lo, number(1, h, C - 1) + 1)
                thin(h, a2_hl, xa).then_inc(l2_tm, 1)
                base(2, h, 0)
                pe.wait_ge(sel_copied, 1)
                pe.wait_ge(t2_uv_lo, h + 1)
                pe.matmul(bank[2 + h][:], sel_r[:, 2], uv[:, h * HT:(h + 1) * HT], start=True,
                          stop=True).then_inc(t2_done, 1)
                base(2, h, 1)
                pe.wait_ge(w12_lo, nth["b2"])
                pe.wait_ge(t2_lo, h + 1)
                delta2(h, 0)
                delta2(h, 1)
                for o in (2, 3):
                    base(2, h, o)
                    delta2(h, o)

            def thin3(h):
                pe.wait_ge(x_lo, number(2, h, C - 1) + 1)
                thin(h, agu_hl, xb).then_inc(l3_tm, 1)

            def sum_ranks(h):
                pe.wait_ge(t3_uv_lo, h + 1)
                if h == 1:
                    pe.wait_ge(t3_lo, 4)
                for g in range(2):
                    ins = pe.matmul(bank[2 + g][:], sel_r[:, g], uv[:, h * HT:(h + 1) * HT], start=True, stop=True)
                ins.then_inc(t3_done, 1)

            def gate_up_main(g, h, slot):
                for c in range(C):
                    hl = wgu_hl[slot]
                    split_product(bank[4 + 2 * h + g][:], hl[:, 0, c, g], hl[:, 1, c, g],
                                  (xb[:, 0, c], xb[:, 1, c]), h, c == 0, False)

            def gate_up_lora(g, h, slot):
                for q in range(2):
                    pair = 2 * h + q
                    ins = pe.matmul(bank[4 + 2 * h + g][:, q * 2 * S:(q + 1) * 2 * S], bgu_st[slot][:, pair, g],
                                    t3_st[:, g, pair * 2 * S:(pair + 1) * 2 * S], start=False, stop=(q == 1))
                ins.then_inc(up_done if g else gate_done, 1)

            pe.wait_ge(w12_lo, nth["agu"])
            thin3(0)
            pe.wait_ge(wgu_lo, 1)
            pe.wait_ge(x_sum, number(2, 0, 0) + 1 + 5)
            gate_up_main(0, 0, 0)
            sum_ranks(0)
            gate_up_main(1, 0, 0)
            thin3(1)
            pe.wait_ge(bgu_ready, 1)
            pe.wait_ge(t3_lo, 4)
            for g in range(2):
                gate_up_lora(g, 0, 0)
            gate_up_main(0, 1, 0)
            sum_ranks(1)
            gate_up_main(1, 1, 0)
            pe.wait_ge(t3_lo, 8)
            for g in range(2):
                gate_up_lora(g, 1, 0)
            with pe.Fori(0, (FC - 1) // 2) as i:
                for u in range(2):
                    fc = 2 * i + 1 + u
                    slot = 1 - u
                    pe.wait_ge(wgu_lo, fc + 1)
                    pe.wait_ge(bgu_ready, fc + 1)
                    for h in range(H):
                        pe.wait_ge(silu_done, 2 * fc - 1 + h)
                        gate_up_main(0, h, slot)
                        gate_up_lora(0, h, slot)
                        pe.wait_ge(act_mul, 2 * fc - 1 + h)
                        gate_up_main(1, h, slot)
                        gate_up_lora(1, h, slot)

            def down_ranks(h):
                pe.wait_ge(act_lo, 2 * FC - 1 + h)
                for j in range(HB):
                    b = HB * h + j
                    for f in range(FC):
                        for k in range(2):
                            ins = pe.matmul(bank[h][0:2 * R, j * S:(j + 1) * S],
                                            ad_hl[:, b, f].rearrange("p k r -> p (k r)"),
                                            act_hl[:, f, k, b * S:(b + 1) * S],
                                            start=(f == 0 and k == 0), stop=(f == FC - 1 and k == 1))
                ins.then_inc(td_tm, 1)

            def down_main(h, i):
                o, cols = DOWN_PIECES[i]
                pe.wait_ge(down_lo, down_nth[f"wd_{o}"])
                if h == 0:
                    pe.wait_ge(act_mul, 2 * FC - 1 + o // 2)
                else:
                    pe.wait_ge(x3_sum, o + 1)
                for f in range(FC):
                    split_product(down_bank(o, cols), wd_hl[o][:, 0, f], wd_hl[o][:, 1, f],
                                  (act_hl[:, f, 0], act_hl[:, f, 1]), h, f == 0, False, cols)

            def down_lora(i):
                o, cols = DOWN_PIECES[i]
                for first in range(cols.start, cols.stop, 2 * S):
                    pair_cols = slice(first, first + 2 * S)
                    dst = down_bank(o, cols)[:, first - cols.start:first - cols.start + 2 * S]
                    ins = pe.matmul(dst, bd_st[:, first // (2 * S), o * P:(o + 1) * P],
                                    td_st[:, pair_cols], start=False, stop=(pair_cols.stop == cols.stop))
                ins.then_inc(down_done, 1)

            pe.wait_ge(ad_lo, 1)
            for h in range(H):
                i = C * h
                down_ranks(h)
                down_main(h, i)
                pe.wait_ge(td_uv_lo, h + 1)
                pe.matmul(bank[2 + h][:], sel_r[0:4 * R, 3], td_uv[h][0:4 * R], start=True,
                          stop=True).then_inc(td_done, 1)
                down_main(h, i + 1)
                pe.wait_ge(down_lo, down_nth["bd"])
                pe.wait_ge(td_lo, 2 * h + 2)
                down_lora(i)
                down_lora(i + 1)
                for i in range(C * h + 2, C if h == 0 else len(DOWN_PIECES)):
                    down_main(h, i)
                    down_lora(i)


def kernel(**inputs):
    import numpy as np
    import concourse.bacc as bacc
    from concourse import mybir as mb
    from concourse.bass_utils import run_bass_kernel_spmd as run

    a = {k: np.asarray(v) for k, v in inputs.items()}

    def chunked(w):
        *lead, k, n = w.shape
        return np.moveaxis(w.reshape(*lead, k // P, P, n), -3, -2)

    def padded(w, axis):
        shape = list(w.shape)
        shape[axis] = FC * P
        z = np.zeros(shape, w.dtype)
        z[tuple(slice(0, n) for n in w.shape)] = w
        return z

    def stacked(w, copies):
        *lead, r, n = w.shape
        return np.broadcast_to(w[..., None, :, :], (*lead, copies, r, n)).reshape(*lead, copies * r, n)

    def rank_sums():
        row, col = np.arange(P)[:, None], np.arange(P)[None]
        gate_up = [(row // R % 2 == g) & (row % R == col % R) for g in range(2)]
        same = np.concatenate([*gate_up, row % R2 == col % R2, row % R == col % R], axis=1)
        return np.concatenate([same * SCALING, -(row // R % 2)], axis=1).astype(np.float32)

    t = lambda w: np.swapaxes(w, -1, -2)
    w_sq = lambda w: chunked(t(w)).reshape(P, C, C, P).transpose(0, 2, 1, 3)
    gu = lambda g, u: np.stack([g, u], axis=-2)
    bg, bu = (padded(t(a[f"L3_cond_B_{n}"][0]), 2).reshape(16, R, FC, P) for n in ("gate", "up"))
    wg, wu = (chunked(padded(t(a[f"L3_cond_W_{n}"]), 1)).reshape(P, C, FC, P) for n in ("gate", "up"))
    arrays = {
        "xT": chunked(t(a["x"])),
        "ids0": a["itok_B_0_15"][None], "ids1": a["itok_B_0_7"], "ids2": a["itok_B_0_4"][None],
        "ids3": a["itok_B_2_6"][None],
        "w0": chunked(t(a["L0_cond_weight"])).reshape(16, P, C * D),
        "w1": w_sq(a["L1_cond_W"]),
        "aw1": chunked(np.concatenate([t(a["L1_cond_A"].reshape(ER, D)), t(a["L1_cond_Wr"])], axis=1)),
        "b1": np.swapaxes(a["L1_cond_B"], 1, 2).reshape(ER, D),
        "w2": w_sq(a["L2_cond_weight"]),
        "a2": chunked(a["L2_cond_lora_A"]),
        "b2": stacked(t(a["L2_cond_lora_B"]), 4),
        "bias2": a["L2_cond_bias"].reshape(C, P).T,
        "wgu": gu(wg, wu).transpose(2, 0, 1, 3, 4),
        "agu": chunked(np.concatenate([t(a["L3_cond_A_gate"][0]), t(a["L3_cond_A_up"][0])], axis=2)),
        "sel": rank_sums(),
        "bgu": stacked(gu(bg, bu).transpose(0, 2, 1, 3, 4).reshape(16, FC, R, 2 * P), 4),
        "wd": chunked(padded(t(a["L3_cond_W_down"]), 0)).reshape(P, FC, C, P).transpose(2, 0, 1, 3),
        "ad": chunked(padded(t(a["L3_cond_A_down"][0]), 1)),
        "bd": stacked(t(a["L3_cond_B_down"][0]), 4),
    }
    nc = bacc.Bacc("TRN2", target_bir_lowering=False, num_devices=1, dynamic_dma_scratch_size=1024)
    feed, args = {}, []
    for name, v in arrays.items():
        v = np.ascontiguousarray(v)
        feed[f"in_{name}"] = v
        args.append(nc.dram_tensor(f"in_{name}", v.shape, mb.dt.from_np(v.dtype), kind="ExternalInput").ap())
    out = nc.dram_tensor("out_0", (C, P, T), mb.dt.float32, kind="ExternalOutput").ap()
    bass_four_residual_layers(nc, *args, out)
    y = run(nc, [feed], core_ids=[0]).results[0]["out_0"]
    return np.ascontiguousarray(y.reshape(D, B, S).transpose(1, 2, 0))
```
